# Optimizing a Trainium2 kernel written in Bass

```python
import numpy as np
import jax
import jax.numpy as jnp

def _softmax(x, axis=-1):
    return jax.nn.softmax(x, axis=axis)

def _gelu(x):
    return jax.nn.gelu(x, approximate=True)

def _silu(x):
    return jax.nn.silu(x)

def _sigmoid(x):
    return jax.nn.sigmoid(x)

def _layernorm(x, axis=-1, eps=1e-05):
    m = jnp.mean(x, axis=axis, keepdims=True)
    v = jnp.var(x, axis=axis, keepdims=True)
    return (x - m) / jnp.sqrt(v + eps)

def _scatter_add(tgt, idx, src, axis=0):
    return tgt.at[idx].add(src)

def _segment_sum(src, seg, n):
    return jax.ops.segment_sum(src, seg, n)
kernel_name = 'mk_gnn_resnorm_d4_gnn_r64_f388a5'

def setup_inputs(seed: int=0):
    np.random.seed(seed)
    _w = jnp.asarray

    def _rec_inputs():
        import jax
        import jax.numpy as jnp
        _gk = jax.random.key(seed)
        x = -0.0003713 + 1 * jax.random.normal(jax.random.fold_in(_gk, 1), (50000, 256), jnp.float32)
        src = jax.random.randint(jax.random.fold_in(_gk, 2), (12500,), 0, 50000, jnp.int32)
        dst = jnp.minimum((50000 * jax.random.uniform(jax.random.fold_in(_gk, 3), (12500,)) ** 2.0).astype(jnp.int32), 49999)
        _o = jnp.argsort(dst, stable=True)
        src = src[_o]
        dst = dst[_o]
        edge_attr_64 = 0.000312547 + 1.00004 * jax.random.normal(jax.random.fold_in(_gk, 12), (12500, 64), jnp.float32)
        return (x, src, dst, edge_attr_64)
    x, src, dst, edge_attr_64 = _rec_inputs()

    def _L0_gnn_setup():
        import jax, jax.numpy as jnp
        import numpy as np
        N_NODES = 50000
        EMB = 256
        HEADS = 8
        NEG_SLOPE = 0.2

        def gat_conv(x, src, dst, W, a_src, a_dst, b, num_nodes):
            h = jnp.einsum('nd,dhf->nhf', x, W)
            al_s = jnp.sum(h * a_src, axis=-1)
            al_d = jnp.sum(h * a_dst, axis=-1)
            logits = jax.nn.leaky_relu(al_s[src] + al_d[dst], NEG_SLOPE)
            m = jax.ops.segment_max(logits, dst, num_segments=num_nodes)
            e = jnp.exp(logits - m[dst])
            z = jax.ops.segment_sum(e, dst, num_segments=num_nodes)
            alpha = e / (z[dst] + 1e-16)
            msg = h[src] * alpha[..., None]
            out = jax.ops.segment_sum(msg, dst, num_segments=num_nodes)
            return out.reshape(num_nodes, -1) + b
        key = jax.random.key(seed)
        ks = jax.random.split(key, 10)
        F1 = EMB // HEADS
        x = jax.random.normal(ks[0], (N_NODES, EMB), dtype=jnp.float32)
        edge_index = jax.random.randint(ks[1], (2, 12500), 0, N_NODES, dtype=jnp.int64)
        s1 = 1.0 / np.sqrt(EMB)
        W1 = jax.random.normal(ks[2], (EMB, HEADS, F1), dtype=jnp.float32) * s1
        a_src1 = jax.random.normal(ks[3], (HEADS, F1), dtype=jnp.float32) * s1
        a_dst1 = jax.random.normal(ks[4], (HEADS, F1), dtype=jnp.float32) * s1
        b1 = jnp.zeros((HEADS * F1,), dtype=jnp.float32)
        W2 = jax.random.normal(ks[5], (EMB, 1, EMB), dtype=jnp.float32) * s1
        a_src2 = jax.random.normal(ks[6], (1, EMB), dtype=jnp.float32) * s1
        a_dst2 = jax.random.normal(ks[7], (1, EMB), dtype=jnp.float32) * s1
        b2 = jnp.zeros((EMB,), dtype=jnp.float32)
        return {'x': x, 'edge_index': edge_index, 'W1': W1, 'a_src1': a_src1, 'a_dst1': a_dst1, 'b1': b1, 'W2': W2, 'a_src2': a_src2, 'a_dst2': a_dst2, 'b2': b2}
    _L0_gnn_all = _L0_gnn_setup()
    _L0_gnn_in = {k: v for k, v in _L0_gnn_all.items() if k in ('W1', 'a_src1', 'a_dst1', 'b1', 'W2', 'a_src2', 'a_dst2', 'b2')}
    del _L0_gnn_all

    def _L1_gnn_setup():
        import jax, jax.numpy as jnp
        import numpy as np
        N_NODES = 50000
        N_EDGES = 12500
        DIM = 256
        HEADS = 8
        DIM_OUT = 32
        key = jax.random.key(seed)
        ks = jax.random.split(key, 9)
        s = 1.0 / np.sqrt(DIM)
        inner = HEADS * DIM_OUT
        return {'x': jax.random.normal(ks[0], (N_NODES, DIM), dtype=jnp.float32), 'Wq': jax.random.uniform(ks[1], (DIM, inner), jnp.float32, -s, s), 'bq': jax.random.uniform(ks[2], (inner,), jnp.float32, -s, s), 'Wk': jax.random.uniform(ks[3], (DIM, inner), jnp.float32, -s, s), 'bk': jax.random.uniform(ks[4], (inner,), jnp.float32, -s, s), 'Wv': jax.random.uniform(ks[5], (DIM, inner), jnp.float32, -s, s), 'bv': jax.random.uniform(ks[6], (inner,), jnp.float32, -s, s), 'src': jax.random.randint(ks[7], (N_EDGES,), 0, N_NODES), 'dst': jax.random.randint(ks[8], (N_EDGES,), 0, N_NODES)}
    _L1_gnn_all = _L1_gnn_setup()
    _L1_gnn_in = {k: v for k, v in _L1_gnn_all.items() if k in ('Wq', 'bq', 'Wk', 'bk', 'Wv', 'bv')}
    del _L1_gnn_all

    def _L2_gnn_setup():
        import jax, jax.numpy as jnp
        import numpy as np
        N, E, H, DE = (10000, 250000, 256, 64)
        EPS = 1e-05

        def _lin_init(k, fan_in, shape):
            s = 1.0 / np.sqrt(fan_in)
            return jax.random.uniform(k, shape, jnp.float32, -s, s)
        key = jax.random.key(seed)
        ks = jax.random.split(key, 12)
        x = jax.random.normal(ks[0], (N, H), jnp.float32)
        edge_index = jax.random.randint(ks[1], (2, E), 0, N)
        edge_attr = jax.random.normal(ks[2], (E, DE), jnp.float32)
        d_in = H + DE
        W1 = _lin_init(ks[3], d_in, (d_in, H))
        b1 = _lin_init(ks[4], d_in, (H,))
        W2 = _lin_init(ks[5], H, (H, H))
        b2 = _lin_init(ks[6], H, (H,))
        Wg = _lin_init(ks[7], d_in, (d_in, H))
        bg = _lin_init(ks[8], d_in, (H,))
        gamma = jnp.ones((H,), jnp.float32)
        beta = jnp.zeros((H,), jnp.float32)
        return {'x': x, 'edge_index': edge_index, 'edge_attr': edge_attr, 'W1': W1, 'b1': b1, 'W2': W2, 'b2': b2, 'Wg': Wg, 'bg': bg, 'gamma': gamma, 'beta': beta}
    _L2_gnn_all = _L2_gnn_setup()
    _L2_gnn_in = {k: v for k, v in _L2_gnn_all.items() if k in ('W1', 'b1', 'W2', 'b2', 'Wg', 'bg', 'gamma', 'beta')}
    del _L2_gnn_all

    def _L3_gnn_setup():
        import jax, jax.numpy as jnp
        import numpy as np
        N_NODES = 50000
        N_EDGES = 12500
        D_IN = 256
        D_HID = 256
        D_OUT = 256
        GAMMA = 0.0
        K_STEPS = 6

        def _spmm(h, src, dst, inv_deg):
            msg = h[src]
            agg = jax.ops.segment_sum(msg, dst, num_segments=h.shape[0])
            return agg * inv_deg[:, None]

        def _linear_diffusion(h, src, dst, gamma=GAMMA, k=K_STEPS):
            n = h.shape[0]
            deg = jax.ops.segment_sum(jnp.ones((src.shape[0],), h.dtype), dst, num_segments=n)
            inv_deg = 1.0 / jnp.clip(deg, 1.0)
            out = h
            term = h
            for i in range(1, k + 1):
                term = (_spmm(term, src, dst, inv_deg) + gamma * term) / float(i)
                out = out + term
            return out
        key = jax.random.key(seed)
        ks = jax.random.split(key, 8)
        h = jax.random.normal(ks[0], (N_NODES, D_IN), dtype=jnp.float32)
        src = jax.random.randint(ks[1], (N_EDGES,), 0, N_NODES, dtype=jnp.int64)
        dst = jax.random.randint(ks[2], (N_EDGES,), 0, N_NODES, dtype=jnp.int64)
        s_in = 1.0 / np.sqrt(D_IN)
        s_hid = 1.0 / np.sqrt(D_HID)
        W_in = jax.random.uniform(ks[3], (D_HID, D_IN), jnp.float32, -s_in, s_in)
        b_in = jax.random.uniform(ks[4], (D_HID,), jnp.float32, -s_in, s_in)
        W_out = jax.random.uniform(ks[5], (D_OUT, D_HID), jnp.float32, -s_hid, s_hid)
        b_out = jax.random.uniform(ks[6], (D_OUT,), jnp.float32, -s_hid, s_hid)
        return {'h': h, 'src': src, 'dst': dst, 'W_in': W_in, 'b_in': b_in, 'W_out': W_out, 'b_out': b_out}
    _L3_gnn_all = _L3_gnn_setup()
    _L3_gnn_in = {k: v for k, v in _L3_gnn_all.items() if k in ('W_in', 'b_in', 'W_out', 'b_out')}
    del _L3_gnn_all
    return {'x': x, 'src': src, 'dst': dst, 'edge_attr_64': edge_attr_64, 'L0_gnn_W1': _L0_gnn_in['W1'], 'L0_gnn_a_src1': _L0_gnn_in['a_src1'], 'L0_gnn_a_dst1': _L0_gnn_in['a_dst1'], 'L0_gnn_b1': _L0_gnn_in['b1'], 'L0_gnn_W2': _L0_gnn_in['W2'], 'L0_gnn_a_src2': _L0_gnn_in['a_src2'], 'L0_gnn_a_dst2': _L0_gnn_in['a_dst2'], 'L0_gnn_b2': _L0_gnn_in['b2'], 'L1_gnn_Wq': _L1_gnn_in['Wq'], 'L1_gnn_bq': _L1_gnn_in['bq'], 'L1_gnn_Wk': _L1_gnn_in['Wk'], 'L1_gnn_bk': _L1_gnn_in['bk'], 'L1_gnn_Wv': _L1_gnn_in['Wv'], 'L1_gnn_bv': _L1_gnn_in['bv'], 'L2_gnn_W1': _L2_gnn_in['W1'], 'L2_gnn_b1': _L2_gnn_in['b1'], 'L2_gnn_W2': _L2_gnn_in['W2'], 'L2_gnn_b2': _L2_gnn_in['b2'], 'L2_gnn_Wg': _L2_gnn_in['Wg'], 'L2_gnn_bg': _L2_gnn_in['bg'], 'L2_gnn_gamma': _L2_gnn_in['gamma'], 'L2_gnn_beta': _L2_gnn_in['beta'], 'L3_gnn_W_in': _L3_gnn_in['W_in'], 'L3_gnn_b_in': _L3_gnn_in['b_in'], 'L3_gnn_W_out': _L3_gnn_in['W_out'], 'L3_gnn_b_out': _L3_gnn_in['b_out']}

def reference(x, src, dst, edge_attr_64, L0_gnn_W1, L0_gnn_a_src1, L0_gnn_a_dst1, L0_gnn_b1, L0_gnn_W2, L0_gnn_a_src2, L0_gnn_a_dst2, L0_gnn_b2, L1_gnn_Wq, L1_gnn_bq, L1_gnn_Wk, L1_gnn_bk, L1_gnn_Wv, L1_gnn_bv, L2_gnn_W1, L2_gnn_b1, L2_gnn_W2, L2_gnn_b2, L2_gnn_Wg, L2_gnn_bg, L2_gnn_gamma, L2_gnn_beta, L3_gnn_W_in, L3_gnn_b_in, L3_gnn_W_out, L3_gnn_b_out):
    import jax
    import jax.numpy as jnp

    def _L0_gnn_ref(x, edge_index, W1, a_src1, a_dst1, b1, W2, a_src2, a_dst2, b2):
        import jax, jax.numpy as jnp
        import numpy as np
        N_NODES = 50000
        EMB = 256
        HEADS = 8
        NEG_SLOPE = 0.2

        def gat_conv(x, src, dst, W, a_src, a_dst, b, num_nodes):
            h = jnp.einsum('nd,dhf->nhf', x, W)
            al_s = jnp.sum(h * a_src, axis=-1)
            al_d = jnp.sum(h * a_dst, axis=-1)
            logits = jax.nn.leaky_relu(al_s[src] + al_d[dst], NEG_SLOPE)
            m = jax.ops.segment_max(logits, dst, num_segments=num_nodes)
            e = jnp.exp(logits - m[dst])
            z = jax.ops.segment_sum(e, dst, num_segments=num_nodes)
            alpha = e / (z[dst] + 1e-16)
            msg = h[src] * alpha[..., None]
            out = jax.ops.segment_sum(msg, dst, num_segments=num_nodes)
            return out.reshape(num_nodes, -1) + b
        n = x.shape[0]
        loops = jnp.arange(n, dtype=edge_index.dtype)
        src = jnp.concatenate([edge_index[0], loops])
        dst = jnp.concatenate([edge_index[1], loops])
        h = gat_conv(x, src, dst, W1, a_src1, a_dst1, b1, n)
        out = gat_conv(h, src, dst, W2, a_src2, a_dst2, b2, n)
        return out

    def _L1_gnn_ref(x, Wq, bq, Wk, bk, Wv, bv, src, dst):
        import jax, jax.numpy as jnp
        import numpy as np
        N_NODES = 50000
        N_EDGES = 12500
        DIM = 256
        HEADS = 8
        DIM_OUT = 32
        n = x.shape[0]
        q = (x @ Wq + bq).reshape(n, HEADS, DIM_OUT)
        k = (x @ Wk + bk).reshape(n, HEADS, DIM_OUT)
        v = (x @ Wv + bv).reshape(n, HEADS, DIM_OUT)
        scores = jnp.einsum('ehd,ehd->eh', q[src], k[dst]) / jnp.sqrt(jnp.asarray(DIM_OUT, dtype=x.dtype))
        m = jax.ops.segment_max(scores, dst, num_segments=n)
        m = jnp.where(jnp.isfinite(m), m, 0.0)
        e = jnp.exp(scores - m[dst])
        z = jax.ops.segment_sum(e, dst, num_segments=n)
        p = e / jnp.maximum(z[dst], 1e-16)
        out = jax.ops.segment_sum(v[src] * p[:, :, None], dst, num_segments=n)
        return out.reshape(n, HEADS * DIM_OUT)

    def _L2_gnn_ref(x, edge_index, edge_attr, W1, b1, W2, b2, Wg, bg, gamma, beta):
        import jax, jax.numpy as jnp
        import numpy as np
        N, E, H, DE = (10000, 250000, 256, 64)
        EPS = 1e-05

        def _lin_init(k, fan_in, shape):
            s = 1.0 / np.sqrt(fan_in)
            return jax.random.uniform(k, shape, jnp.float32, -s, s)
        src, dst = (edge_index[0], edge_index[1])
        ei = jnp.concatenate([x[src], edge_attr], axis=-1)
        core = jnp.maximum(ei @ W1 + b1, 0.0) @ W2 + b2
        gate = jax.nn.sigmoid(ei @ Wg + bg)
        msg = gate * core
        agg = jax.ops.segment_sum(msg, dst, num_segments=x.shape[0])
        out = agg + x
        mu = jnp.mean(out, axis=-1, keepdims=True)
        var = jnp.var(out, axis=-1, keepdims=True)
        out = (out - mu) * jax.lax.rsqrt(var + EPS) * gamma + beta
        return out

    def _L3_gnn_ref(h, src, dst, W_in, b_in, W_out, b_out):
        import jax, jax.numpy as jnp
        import numpy as np
        N_NODES = 50000
        N_EDGES = 12500
        D_IN = 256
        D_HID = 256
        D_OUT = 256
        GAMMA = 0.0
        K_STEPS = 6

        def _spmm(h, src, dst, inv_deg):
            msg = h[src]
            agg = jax.ops.segment_sum(msg, dst, num_segments=h.shape[0])
            return agg * inv_deg[:, None]

        def _linear_diffusion(h, src, dst, gamma=GAMMA, k=K_STEPS):
            n = h.shape[0]
            deg = jax.ops.segment_sum(jnp.ones((src.shape[0],), h.dtype), dst, num_segments=n)
            inv_deg = 1.0 / jnp.clip(deg, 1.0)
            out = h
            term = h
            for i in range(1, k + 1):
                term = (_spmm(term, src, dst, inv_deg) + gamma * term) / float(i)
                out = out + term
            return out
        x = h @ W_in.T + b_in
        x = jax.nn.silu(x)
        x = _linear_diffusion(x, src, dst)
        x = x @ W_out.T + b_out
        return x
    edge_index = jnp.stack([src, dst])
    x = _layernorm(x + _L0_gnn_ref(x, edge_index, L0_gnn_W1, L0_gnn_a_src1, L0_gnn_a_dst1, L0_gnn_b1, L0_gnn_W2, L0_gnn_a_src2, L0_gnn_a_dst2, L0_gnn_b2), axis=-1)
    x = _layernorm(x + _L1_gnn_ref(x, L1_gnn_Wq, L1_gnn_bq, L1_gnn_Wk, L1_gnn_bk, L1_gnn_Wv, L1_gnn_bv, src, dst), axis=-1)
    x = _layernorm(x + _L2_gnn_ref(x, edge_index, edge_attr_64, L2_gnn_W1, L2_gnn_b1, L2_gnn_W2, L2_gnn_b2, L2_gnn_Wg, L2_gnn_bg, L2_gnn_gamma, L2_gnn_beta), axis=-1)
    x = _layernorm(x + _L3_gnn_ref(x, src, dst, L3_gnn_W_in, L3_gnn_b_in, L3_gnn_W_out, L3_gnn_b_out), axis=-1)
    return x

_drawn_inputs = setup_inputs


def setup_inputs(seed=0):
    import zlib

    import numpy as np

    out = dict(_drawn_inputs(seed))
    spreads = {'L0_gnn_b1': (0.0, 0.1),
     'L0_gnn_b2': (0.0, 0.1),
     'L2_gnn_gamma': (1.0, 0.2),
     'L2_gnn_beta': (0.0, 0.1)}
    factors = {'edge_attr_64': 4.381,
     'L0_gnn_a_src1': 2.936,
     'L0_gnn_a_dst1': 7.931,
     'L0_gnn_a_dst2': 14.792,
     'L1_gnn_Wq': 3.862,
     'L1_gnn_bq': 64.0,
     'L1_gnn_Wk': 3.902,
     'L1_gnn_bk': 43.278,
     'L1_gnn_bv': 3.861,
     'L2_gnn_b1': 29.732,
     'L2_gnn_b2': 8.0,
     'L2_gnn_Wg': 6.794,
     'L2_gnn_bg': 64.0,
     'L3_gnn_b_in': 3.903}
    for name, (base, spread) in spreads.items():
        noise = np.random.default_rng([zlib.crc32(name.encode()), seed]).standard_normal(out[name].shape)
        drawn = base * np.exp(spread * noise) if base else spread * noise
        out[name] = jnp.asarray(drawn.astype(out[name].dtype))
    for name, factor in factors.items():
        out[name] = (out[name] * factor).astype(out[name].dtype)
    return out
```

```python
from contextlib import ExitStack, contextmanager

import numpy as np
import concourse.bass as bass
from concourse import mybir

P = 128
F32 = mybir.dt.float32
I32 = mybir.dt.int32
ALU = mybir.AluOpType
ACT = mybir.ActivationFunctionType
AXX = mybir.AxisListType.X
BIG = 1e30
EPS = 1e-5
OFF_TABLE = 65536.0
STEPS = 6


class Stage:

    count = 0

    def __init__(self, nc):
        self.nc, self.sems, self.ctx = nc, [], ExitStack()
        Stage.count += 1
        self.tag = f"s{Stage.count}_"

    def __enter__(self):
        return self

    def sb(self, name, shape, dt=F32, n=None):
        if n is None:
            return self.ctx.enter_context(self.nc.sbuf_tensor(self.tag + name, shape, dt))
        return [self.ctx.enter_context(self.nc.sbuf_tensor(f"{self.tag}{name}{i}", shape, dt)) for i in range(n)]

    def ps(self, name, n):
        return [self.ctx.enter_context(self.nc.psum_tensor(f"{self.tag}{name}{i}", [P, 512], F32)) for i in range(n)]

    def sem(self, name, n=None):
        got = [self.nc.alloc_semaphore(self.tag + (name if n is None else f"{name}{i}")) for i in range(n or 1)]
        self.sems += got
        return got[0] if n is None else got

    def __exit__(self, *e):
        self.ctx.close()
        if e[0] is None:
            self.nc.clear_and_free_semaphores(self.sems)
            self.nc.all_engine_barrier()


def upto(sems, u, j, back=0, inc=1):
    n = len(sems)
    assert back <= n
    return sems[(u - back) % n], (j + 1 if u >= back else j + 0) * inc


class Chain:

    def __init__(self, eng, sem, per=None, turn=0):
        self.eng, self.sem, self.per = eng, sem, per
        self.base, self.k = (0 if per is None else turn * per), 0

    def __call__(self, ins):
        ins.then_inc(self.sem, 1)
        self.k += 1

    def wait(self):
        self.eng.wait_ge(self.sem, self.base + self.k)

    def close(self):
        assert self.k == self.per, (self.k, self.per)


def heads(ap, h):
    return ap.rearrange("p (h j) -> p h j", h=h)


def col(ap, t):
    return ap[:, bass.ds(t, 1)]


def tile_of(tab, t):
    return tab[bass.ds(t, 1)].rearrange("o p d -> (o p) d")


class Net:

    def __init__(self, nc, a, ctx):
        self.nc, self.a = nc, a
        self.N, self.D = a["x"].shape
        self.T = T = a["key_rows"].shape[0]
        self.R = R = T * P
        self.H, self.DE = 8, a["edge_attr_t"].shape[0]
        D, H = self.D, self.H
        self.C = C = D // P
        assert T % 4 == 0 and T <= P and C == 2 and self.N < OFF_TABLE
        dram = lambda name, shape, dt=F32: nc.dram_tensor(name, shape, dt).ap()
        self.proj1 = dram("proj1", [T, P, 4 * D])
        self.out1 = dram("out1", [2 * R, D])
        self.out1_src = dram("out1_src", [T, P, D])
        self.x1 = dram("x1", [2 * R, D])
        self.v_edge = dram("v_edge", [T, P, D])
        self.x2 = dram("x2", [2 * R, D])
        self.msg = dram("msg", [T, P, D])
        self.x3 = dram("x3", [T, P, D])
        self.h = dram("h", [2 * R, D])
        self.term = [dram(f"term{i}", [R + P, D]) for i in range(2)]
        self.rep = dram("rep", [self.N, 1], I32)

        sb = lambda name, shape, dt=F32: ctx.enter_context(nc.sbuf_tensor(name, shape, dt))
        self.w1x = sb("w1x", [P, C, D + 3 * H])
        self.w2 = sb("w2", [P, C, D])
        self.w12 = sb("w12", [P, C, D])
        self.w_qv = sb("w_qv", [P, C, 2 * D])
        self.w_k = sb("w_k", [P, C, D])
        self.w_m1 = sb("w_m1", [P, C, D])
        self.w_m1e = sb("w_m1e", [self.DE, D])
        self.w_g = sb("w_g", [P, C, D])
        self.w_ge = sb("w_ge", [self.DE, D])
        self.w_m2 = sb("w_m2", [P, C, D])
        self.w_in = sb("w_in", [P, C, D])
        self.w_out = sb("w_out", [P, C, D])
        self.bc_names = ["b1", "b2", "gamma", "beta", "b_out", "a_src1", "a_dst1", "a_src2", "a_dst2"]
        self.bc = {n: sb(f"{n}_bc", [P, D]) for n in self.bc_names}
        self.c12 = sb("c12", [P, D])
        self.att2 = sb("att2", [P, 2, D])
        self.row_names = ["b_in"]
        self.rows1 = sb("rows1", [1, 1, D])
        self.col_names = ["b1", "bm1", "b_in"]
        self.cols = sb("cols", [P, 3, C])
        self.ident = sb("ident", [P, P])
        self.ones = sb("ones", [P, P])
        self.neg_half = sb("neg_half", [P, 8])
        self.index = sb("index", [P, T, 2], I32)
        self.key_in = sb("key_in", [P, T])
        self.lower = sb("lower", [T, T])
        self.upper = sb("upper", [T, T])
        self.pen_lower = sb("pen_lower", [T, T])
        self.pen_upper = sb("pen_upper", [T, T])
        self.same = sb("same", [T, H * P])
        self.pen_same = sb("pen_same", [T, H * P])
        self.first = sb("first", [T, P])
        self.last = sb("last", [T, P])
        self.pen_first = sb("pen_first", [T, P])
        self.pen_last = sb("pen_last", [T, P])
        self.is_rep = sb("is_rep", [T, P])
        self.pos = sb("pos", [P, T])
        self.pos_i = sb("pos_i", [P, T], I32)
        self.rep_node = sb("rep_node", [P, T], I32)
        self.dst_row = sb("dst_row", [P, T], I32)
        self.src_rep = sb("src_rep", [P, T])
        self.table_row = sb("table_row", [P, T], I32)
        self.term_row = sb("term_row", [P, T], I32)
        self.inv_deg = sb("inv_deg", [P, T])
        self.dots2 = sb("dots2", [P, 3, T])
        self.scores = sb("scores", [P, 2 * H, T])
        self.passed = nc.alloc_semaphore("waits_passed")


def hold(net, eng, sem, value):
    eng.wait_ge(sem, value)
    eng.sem_inc(net.passed, 1)


class Segments:

    def __init__(self, net, st):
        T, H = net.T, net.H
        self.net, self.T = net, T
        self.fwd = st.sb("seg_fwd", [T, H * P])
        self.bwd = st.sb("seg_bwd", [T, H * P])
        self.diag = st.sb("seg_diag", [T, 2, H, T])
        self.ends = st.sb("seg_ends", [T, 2, H])
        self.cross = st.sb("seg_cross", [T, 2, H])
        self.ask = st.sem("seg_ask")
        self.got = st.sem("seg_got")
        self.bank = st.ps("seg_bank", 4)
        self.asked = 0
        self.given = 0

    def cross_pe(self, pe, n, is_max):
        T, net, nc, bank = self.T, self.net, self.net.nc, self.bank
        self.given += 1
        pe.wait_ge(self.ask, self.given)
        if not is_max:
            nc.tensor.matmul(bank[0][0:T, 0:n], net.upper[:], self.ends[:, 0, 0:n], start=True, stop=True)
            mm = nc.tensor.matmul(bank[2][0:T, 0:n], net.lower[:], self.ends[:, 1, 0:n], start=True, stop=True)
        else:
            m = (n + 1) // 2
            for i in range(2):
                for half in range(2 if n > 1 else 1):
                    mm = nc.tensor.matmul(bank[2 * i + half][0:T, 0:m * T], net.ones[0:T, 0:T],
                                          self.diag[:, i, half * m:(half + 1) * m, :].rearrange("p h c -> p (h c)"), start=True, stop=True)
        mm.then_inc(self.got, 1)

    def _ask(self, ch):
        ch.wait()
        ch.eng.sem_inc(self.ask, 1)
        self.asked += 1
        ch.eng.wait_ge(self.got, self.asked)

    def sum_dve(self, ch, tot, val, n):
        T, net, nc, m = self.T, self.net, self.net.nc, n * P
        V = nc.vector
        ch.wait()
        ch(V.memset(self.bwd[:, m - 1:m], 0.0))
        ch(V.tensor_tensor_scan(self.fwd[:, 0:m], net.same[:, 0:m], val[:, 0:m], 0.0, ALU.mult, ALU.add))
        ch(V.tensor_tensor_scan(self.bwd[:, 0:m - 1][:, ::-1], val[:, 1:m][:, ::-1], net.same[:, 1:m][:, ::-1], 0.0, ALU.add, ALU.mult))
        ch.wait()
        ch(V.tensor_tensor(tot[:, 0:m], self.fwd[:, 0:m], self.bwd[:, 0:m], ALU.add))
        ch.wait()
        t3 = heads(tot[:, 0:m], n)
        for i, c in enumerate((P - 1, 1)):
            ch(V.tensor_copy(self.ends[:, i, 0:n], t3[:, :, c]))
        self._ask(ch)
        for i in range(2):
            ch(V.tensor_copy(self.cross[:, i, 0:n], self.bank[2 * i][0:T, 0:n]))
        ch.wait()
        for buf, i, mask in ((self.fwd, 0, net.first), (self.bwd, 1, net.last)):
            ch(V.tensor_tensor(heads(buf[:, 0:m], n), mask[:].unsqueeze(1).broadcast_to([T, n, P]),
                               self.cross[:, i, 0:n].unsqueeze(2).broadcast_to([T, n, P]), ALU.mult))
        for buf in (self.fwd, self.bwd):
            ch.wait()
            ch(V.tensor_tensor(tot[:, 0:m], tot[:, 0:m], buf[:, 0:m], ALU.add))

    def max_dve(self, ch, tot, val, n):
        T, net, nc, m = self.T, self.net, self.net.nc, n * P
        V = nc.vector
        ch.wait()
        ch(V.tensor_copy(self.bwd[:, m - 1:m], val[:, m - 1:m]))
        ch(V.tensor_tensor_scan(self.fwd[:, 0:m], net.pen_same[:, 0:m], val[:, 0:m], -BIG, ALU.add, ALU.max))
        ch(V.tensor_tensor_scan(self.bwd[:, 0:m - 1][:, ::-1], net.pen_same[:, 1:m][:, ::-1], val[:, 0:m - 1][:, ::-1],
                                val[:, m - 1:m], ALU.add, ALU.max))
        ch.wait()
        ch(V.tensor_tensor(tot[:, 0:m], self.fwd[:, 0:m], self.bwd[:, 0:m], ALU.max))
        ch.wait()
        t3 = heads(tot[:, 0:m], n)
        for i, c in enumerate((P - 1, 1)):
            ch(V.tensor_tensor(self.diag[:, i, 0:n, :], net.ident[0:T, 0:T].unsqueeze(1).broadcast_to([T, n, T]),
                               t3[:, :, c:c + 1].broadcast_to([T, n, T]), ALU.mult))
        self._ask(ch)
        half = (n + 1) // 2
        for i, pen in enumerate((net.pen_lower, net.pen_upper)):
            for q in range(2 if n > 1 else 1):
                ch(V.tensor_tensor(self.diag[:, i, q * half:(q + 1) * half, :],
                                   self.bank[2 * i + q][0:T, 0:half * T].rearrange("p (h c) -> p h c", h=half),
                                   pen[:].unsqueeze(1).broadcast_to([T, half, T]), ALU.add))
        ch.wait()
        for i in range(2):
            ch(V.tensor_reduce(self.cross[:, i, 0:n], self.diag[:, i, 0:n, :], AXX, ALU.max))
        ch.wait()
        for buf, i, pen in ((self.fwd, 0, net.pen_first), (self.bwd, 1, net.pen_last)):
            ch(V.tensor_tensor(heads(buf[:, 0:m], n), pen[:].unsqueeze(1).broadcast_to([T, n, P]),
                               self.cross[:, i, 0:n].unsqueeze(2).broadcast_to([T, n, P]), ALU.add))
        for buf in (self.fwd, self.bwd):
            ch.wait()
            ch(V.tensor_tensor(tot[:, 0:m], tot[:, 0:m], buf[:, 0:m], ALU.max))


def setup(net):
    nc, a, T, D, H, C, N, R = net.nc, net.a, net.T, net.D, net.H, net.C, net.N, net.R
    with Stage(nc) as st:
        key_in_i = st.sb("key_in_i", [P, T], I32)
        key_int = st.sb("key_int", [T, P + 1], I32)
        key = st.sb("key", [T, P + 1])
        pos_row_i = st.sb("pos_row_i", [T, P], I32)
        pos_row = st.sb("pos_row", [T, P])
        fill = st.sb("fill", [125, N // 125], I32)
        zeros = st.sb("zeros", [P, D])
        prod = st.sb("prod", [P, D])
        rep_col = st.sb("rep_col", [P, D])
        w1t = st.sb("w1t", [P, C, D])
        att_col = st.sb("att_col", [P, 2, C])
        diag = st.sb("diag", [T, 2, T])
        val = st.sb("val", [T, 2 * P])
        tot = st.sb("tot", [T, 2 * P])
        node = st.sb("node", [T, P])
        as_col = st.sb("as_col", [P, 3, T])
        loaded = st.sem("loaded")
        pool_chain = st.sem("pool_chain")
        masks = st.sem("triangles_ready")
        const_ready = st.sem("const_ready")
        clear = st.sem("tables_cleared")
        w1t_ready = st.sem("w1t_ready")
        transposed = st.sem("transposed")
        folded = st.sem("folded")
        ends_ready = st.sem("ends_ready")
        chain = st.sem("dve_chain")
        b1_ready = st.sem("b1_ready")
        v_ready = st.sem("v_ready")
        v_used = st.sem("v_used")
        diag_ready = st.sem("diag_ready")
        rows_ready = st.sem("rows_ready")
        cols_ready = st.sem("cols_ready")
        seg = Segments(net, st)
        bank = st.ps("setup_bank", 4)
        block = st.ctx.enter_context(nc.Block())
        chunks = lambda ap: ap.rearrange("(c p) d -> p c d", p=P)
        loads = [
            (net.index[:], a["index_cols"]), (key_in_i[:], a["key_in_cols"]), (key_int[:], a["key_rows"]),
            (net.w1x[:, :, 0:D], chunks(a["w1"])), (net.w2[:], chunks(a["w2"])),
            (net.w_qv[:, :, 0:D], chunks(a["wq"])), (net.w_qv[:, :, D:2 * D], chunks(a["wv"])), (net.w_k[:], chunks(a["wk"])),
            (net.w_m1[:], chunks(a["wm1"][0:D, :])), (net.w_m1e[:], a["wm1"][D:D + net.DE, :]),
            (net.w_g[:], chunks(a["wg"][0:D, :])), (net.w_ge[:], a["wg"][D:D + net.DE, :]),
            (net.w_m2[:], chunks(a["wm2"])), (net.w_in[:], chunks(a["w_in_t"])), (net.w_out[:], chunks(a["w_out_t"])),
        ]
        loads += [(net.bc[n][:], a[n].partition_broadcast(P)) for n in net.bc_names]
        loads += [(net.rows1[:, i, :], a[n].unsqueeze(0)) for i, n in enumerate(net.row_names)]
        loads += [(net.cols[:, i, :], a[n].rearrange("(c p) -> p c", p=P)) for i, n in enumerate(net.col_names)]

        @block.sync
        def _(sp):
            with nc.allow_non_contiguous_dma("three biases as columns, once"):
                for dst, src in loads:
                    sp.dma_start(dst, src).then_inc(loaded, 16)

        @block.gpsimd
        def _(gp):
            ch = Chain(gp, pool_chain)
            ch(nc.gpsimd.memset(net.ones[:], 1.0))
            ch(nc.gpsimd.memset(net.neg_half[:], -0.5))
            ch(nc.gpsimd.memset(net.ident[:], 0.0))
            ch(nc.gpsimd.iota(net.pos_i[:], pattern=[[P, T]], base=0, channel_multiplier=1))
            ch(nc.gpsimd.iota(pos_row_i[:], pattern=[[1, P]], base=0, channel_multiplier=P))
            ch(nc.gpsimd.memset(fill[:], -1))
            ch(nc.gpsimd.memset(zeros[:], 0.0))
            ch.wait()
            nc.gpsimd.affine_select(out=net.ident[:], in_=net.ident[:], compare_op=ALU.not_equal, fill=1.0, base=0,
                                    pattern=[[-1, P]], channel_multiplier=1).then_inc(const_ready, 1)
            nc.gpsimd.affine_select(out=net.lower[:], in_=net.ones[0:T, 0:T], compare_op=ALU.is_gt, fill=0.0, base=0,
                                    pattern=[[-1, T]], channel_multiplier=1).then_inc(masks, 1)
            nc.gpsimd.affine_select(out=net.upper[:], in_=net.ones[0:T, 0:T], compare_op=ALU.is_gt, fill=0.0, base=0,
                                    pattern=[[1, T]], channel_multiplier=-1).then_inc(masks, 1)
            gp.dma_start(net.rep.rearrange("(p a) o -> p (a o)", p=125), fill[:]).then_inc(clear, 16)
            for tab in net.term:
                gp.dma_start(tab[R:R + P, :], zeros[:]).then_inc(clear, 16)
            gp.wait_ge(clear, 48)

        @block.tensor
        def _(pe):
            pe.wait_ge(loaded, 16 * len(loads))
            pe.wait_ge(const_ready, 1)
            for m in range(C):
                for c in range(C):
                    mm = nc.tensor.transpose(bank[m][:, c * P:(c + 1) * P], net.w1x[:, c, m * P:(m + 1) * P], net.ident[:])
            mm.then_inc(transposed, 1)
            pe.wait_ge(w1t_ready, 1)
            for c in range(C):
                for m in range(C):
                    mm = nc.tensor.matmul(bank[2 + c][:, 0:D], w1t[:, m, c * P:(c + 1) * P], net.w2[:, m, :], start=m == 0, stop=m == C - 1)
            mm.then_inc(transposed, 1)
            pe.wait_ge(b1_ready, 1)
            for c in range(C):
                mm = nc.tensor.matmul(bank[0][:, 0:D], rep_col[:, c * P:(c + 1) * P], net.w2[:, c, :], start=c == 0, stop=c == C - 1)
            mm.then_inc(folded, 1)
            for k in range(2):
                pe.wait_ge(v_ready, k + 1)
                for c in range(C):
                    mm = nc.tensor.matmul(bank[1][:, c * P:(c + 1) * P], rep_col[:, c * P:(c + 1) * P], net.ident[:], start=True, stop=True)
                mm.then_inc(folded, 1)
                pe.wait_ge(v_used, k + 1)
            pe.wait_ge(diag_ready, 1)
            nc.tensor.matmul(bank[0][0:T, 0:2 * T], net.ones[0:T, 0:T], diag[:].rearrange("p k c -> p (k c)"), start=True, stop=True).then_inc(ends_ready, 1)
            seg.cross_pe(pe, 2, False)
            pe.wait_ge(rows_ready, 1)
            for k, src in enumerate((node[:], tot[:, 0:P], tot[:, P:2 * P])):
                mm = nc.tensor.transpose(bank[1][:, k * T:(k + 1) * T], src, net.ident[0:T, 0:T])
            mm.then_inc(cols_ready, 1)

        @block.scalar
        def _(act):
            act.wait_ge(transposed, 1)
            for m in range(C):
                mv = nc.scalar.activation(w1t[:, m, :], bank[m][:, 0:D], ACT.Copy)
            mv.then_inc(w1t_ready, 1)
            act.wait_ge(transposed, 2)
            for c in range(C):
                nc.scalar.activation(net.w12[:, c, :], bank[2 + c][:, 0:D], ACT.Copy)

        @block.vector
        def _(dve):
            V = nc.vector
            ch = Chain(dve, chain)
            dve.wait_ge(loaded, 16 * len(loads))
            dve.wait_ge(const_ready, 1)
            ch(V.tensor_copy(rep_col[:, 0:P], net.cols[:, 0, 0:1].broadcast_to([P, P])))
            V.tensor_copy(rep_col[:, P:2 * P], net.cols[:, 0, 1:2].broadcast_to([P, P])).then_inc(b1_ready, 1)
            for c in range(C):
                w = net.w1x[:, c, :]
                for name, at in (("a_dst1", D), ("a_src1", D + 2 * H)):
                    ch.wait()
                    ch(V.tensor_tensor(prod[:], w[:, 0:D], net.bc[name][:], ALU.mult))
                    ch.wait()
                    ch(V.tensor_reduce(w[:, at:at + H], heads(prod[:], H), AXX, ALU.add))
                ch.wait()
                ch(V.tensor_tensor(w[:, D + H:D + 2 * H], w[:, D:D + H], w[:, D + 2 * H:D + 3 * H], ALU.add))
            for k, name in enumerate(("a_src2", "a_dst2")):
                for c in range(C):
                    ch.wait()
                    ch(V.tensor_tensor(prod[:], net.w2[:, c, :], net.bc[name][:], ALU.mult))
                    ch.wait()
                    ch(V.tensor_reduce(att_col[:, k, c:c + 1], prod[:], AXX, ALU.add))
            dve.wait_ge(folded, 1)
            ch(V.tensor_tensor(net.c12[:], bank[0][:, 0:D], net.bc["b2"][:], ALU.add))
            for k in range(2):
                ch.wait()
                for c in range(C):
                    ch(V.tensor_copy(rep_col[:, c * P:(c + 1) * P], att_col[:, k, c:c + 1].broadcast_to([P, P])))
                ch.wait()
                dve.sem_inc(v_ready, 1)
                dve.wait_ge(folded, k + 2)
                V.tensor_copy(net.att2[:, k, :], bank[1][:, 0:D]).then_inc(v_used, 1)
            ch(V.tensor_copy(net.key_in[:], key_in_i[:]))
            ch(V.tensor_copy(key[:], key_int[:]))
            ch(V.tensor_copy(net.pos[:], net.pos_i[:]))
            ch(V.tensor_copy(pos_row[:], pos_row_i[:]))
            ch.wait()
            ch(V.tensor_scalar(diag[:, 0, :], net.ident[0:T, 0:T], key[:, 1:2], None, ALU.mult))
            ch(V.tensor_scalar(diag[:, 1, :], net.ident[0:T, 0:T], key[:, P - 1:P], None, ALU.mult))
            ch.wait()
            dve.sem_inc(diag_ready, 1)
            same = heads(net.same[:], H)
            ch(V.tensor_tensor(same[:, :, 2:P], key[:, 2:P].unsqueeze(1).broadcast_to([T, H, P - 2]),
                               key[:, 1:P - 1].unsqueeze(1).broadcast_to([T, H, P - 2]), ALU.is_equal))
            ch(V.memset(same[:, :, 0:2], 0.0))
            ch(V.tensor_scalar(net.first[:], key[:, 0:P], key[:, 1:2], None, ALU.is_equal))
            ch(V.tensor_scalar(net.last[:], key[:, 0:P], key[:, P - 1:P], None, ALU.is_equal))
            ch(V.tensor_tensor(net.is_rep[:], key[:, 0:P], key[:, 1:P + 1], ALU.not_equal))
            ch.wait()
            for m in (net.first, net.last, net.is_rep):
                ch(V.memset(m[:, 0:1], 0.0))
            dve.wait_ge(ends_ready, 1)
            dve.wait_ge(masks, 2)
            ch(V.scalar_tensor_tensor(net.lower[:], bank[0][0:T, T:2 * T], key[:, 1:2], net.lower[:], ALU.is_equal, ALU.mult))
            ch(V.scalar_tensor_tensor(net.upper[:], bank[0][0:T, 0:T], key[:, P - 1:P], net.upper[:], ALU.is_equal, ALU.mult))
            ch.wait()
            for pen, m in ((net.pen_lower, net.lower), (net.pen_upper, net.upper), (net.pen_same, net.same),
                           (net.pen_first, net.first), (net.pen_last, net.last)):
                ch(V.tensor_scalar(pen[:], m[:], -1.0, BIG, ALU.add, ALU.mult))
            ch(V.memset(val[:, 0:P], 1.0))
            ch(V.tensor_tensor(val[:, P:2 * P], pos_row[:], net.is_rep[:], ALU.mult))
            ch(V.tensor_scalar(node[:], key[:, 0:P], -OFF_TABLE, None, ALU.add))
            ch.wait()
            ch(V.memset(val[:, 0:1], 0.0))
            ch(V.tensor_tensor(node[:], node[:], net.is_rep[:], ALU.mult))
            ch.wait()
            ch(V.tensor_scalar(node[:], node[:], OFF_TABLE, None, ALU.add))
            seg.sum_dve(ch, tot, val, 2)
            ch.wait()
            dve.sem_inc(rows_ready, 1)
            dve.wait_ge(cols_ready, 1)
            ch(V.tensor_copy(net.rep_node[:], bank[1][:, 0:T]))
            ch(V.tensor_copy(net.dst_row[:], bank[1][:, 2 * T:3 * T]))
            ch(V.tensor_scalar(net.inv_deg[:], bank[1][:, T:2 * T], 1.0, None, ALU.max))
            ch.wait()
            V.reciprocal(net.inv_deg[:], net.inv_deg[:])


def ln_stats(net, dve, chain, j, S, ready, parts, var, slots=None):
    V = net.nc.vector
    slots = range(len(chain)) if slots is None else slots
    n = len(parts(0))
    chs = {u: Chain(dve, chain[u], 2 * n + 1, j) for u in slots}
    for u in slots:
        ready(u)
        for i, x in enumerate(parts(u)):
            chs[u](V.bn_stats(S[u][:, 24 + 6 * i:30 + 6 * i], x))
    for u in slots:
        hold(net, dve, chs[u].sem, chs[u].base + chs[u].k)
        for i in range(n):
            chs[u](V.bn_aggr(S[u][:, 2 * i:2 * i + 2], S[u][:, 24 + 6 * i:30 + 6 * i]))
    for u in slots:
        chs[u].wait()
        chs[u](V.tensor_scalar(S[u][:, 8:8 + n], S[u][:, 0:2 * n:2], -1.0, None, ALU.mult))
        V.tensor_scalar(S[u][:, 16:16 + n], S[u][:, 1:2 * n:2], EPS, None, ALU.add).then_inc(var[u], 1)
        chs[u].close()


def inv_dev(net, s, n):
    return net.nc.gpsimd.tensor_tensor(s[:, 20:20 + n], s[:, 16:16 + n], net.neg_half[:, 0:n], ALU.pow)


def dev_shift(net, gp, s, n, dev, shift, value):
    inv_dev(net, s, n).then_inc(dev, 1)
    hold(net, gp, dev, value)
    net.nc.gpsimd.tensor_tensor(s[:, 12:12 + n], s[:, 8:8 + n], s[:, 20:20 + n], ALU.mult).then_inc(shift, 1)


def normed_act(net, out, x, s, i):
    return net.nc.scalar.activation(out, x, ACT.Identity, bias=s[:, 12 + i:13 + i], scale=s[:, 20 + i:21 + i])


def normed(net, out, x, s, i):
    return net.nc.vector.tensor_scalar(out, x, s[:, 2 * i:2 * i + 1], s[:, 20 + i:21 + i], ALU.subtract, ALU.mult)


def dense(net):
    nc, a, D, C, N = net.nc, net.a, net.D, net.C, net.N
    G = 4
    BR = G * P
    NB = -(-N // BR)
    assert NB % 2 == 0 and NB >= 6 and N >= BR
    LAST = NB // 2 - 1
    with Stage(nc) as st:
        X = st.sb("n_x", [P, G, D], n=2)
        XB = st.sb("n_x_biased", [P, G, D], n=2)
        B = st.sb("n_biased", [P, G, D], n=2)
        Y = st.sb("n_y", [P, G, D], n=2)
        Z = st.sb("n_z", [P, G, D], n=2)
        W = st.sb("n_w", [P, G, D], n=2)
        O = st.sb("n_o", [P, G, D], n=2)
        XT = st.sb("n_xt", [P, C, 2 * P], n=2)
        X3T = st.sb("n_x3t", [P, C, 2 * P], n=2)
        HT = st.sb("n_ht", [P, C, 2 * P], n=2)
        S = st.sb("n_small", [P, 128], n=2)
        x_in, x_biased, var1, scaled, x2_ready, x2_biased, var3, dev3, x3_ready, x3_biased, var5, dev5, shift5, o_ready, stored = (
            st.sem(f"n_{n}", 2) for n in (
                "x_loaded", "x_biased", "var1_ready", "scales_ready", "x2_ready", "x2_biased", "var3_ready", "dev3_ready", "x3_ready",
                "x3_biased", "var5_ready", "dev5_ready", "shift5_ready", "out_ready", "stored"))
        pr, y_ready, hid, silu, outp, y5 = (
            st.sem(f"n_{n}", 2) for n in ("projected", "y_ready", "hidden", "silu_ready", "out_projected", "y5_ready"))
        xt_made, xt_moved, x3t_made, x3t_moved = (st.sem(f"n_{n}") for n in ("xt_made", "xt_moved", "x3t_made", "x3t_moved"))
        shift3 = st.sem("n_shift3_ready", 2)
        chain1, chain3, chain6 = (st.sem(f"n_dve_chain{i}", 2) for i in (1, 3, 6))
        tps, prs, hds, ops = (st.ps(f"n_ps_{n}", 2) for n in ("t", "p", "h", "o"))
        slot = st.sb("n_rep_slot", [P, 2], I32, n=2)
        slot_ready, rep_stored = st.sem("n_rep_slot_ready", 2), st.sem("n_rep_stored", 2)
        assert 2 * LAST <= net.T
        block = st.ctx.enter_context(nc.Block())

        def ahead(j, u, d):
            return j + (u + d) // 2, (u + d) % 2

        def start_of(j, u):
            return N - BR if isinstance(j, int) and j == LAST and u == 1 else j * (2 * BR) + u * BR

        def rows_of(tab, start):
            return tab[bass.ds(start, BR), :].rearrange("(p g) d -> p g d", g=G)

        half = lambda buf, u, h: buf[u][:, 2 * h:2 * h + 2, :].rearrange("p g d -> p (g d)")

        @block.sync
        def _(sp):
            def load(start, u):
                sp.dma_start(X[u][:], rows_of(a["x"], start)).then_inc(x_in[u], 16)

            def load_next(j, u, start):
                hold(net, sp, xt_made, j * 4 + (2 * u + 2))
                hold(net, sp, x_biased[u], j + 1)
                load(start, u)
            for u in range(2):
                load(u * BR, u)
            with sp.Fori(0, LAST - 1) as j:
                for u in range(2):
                    load_next(j, u, j * (2 * BR) + (2 + u) * BR)
            for u in range(2):
                load_next(LAST - 1, u, start_of(LAST, u))

        @block.gpsimd
        def _(gp):
            G_ = nc.gpsimd

            def bias(out, src, row):
                return G_.tensor_tensor(out, src, row[:].unsqueeze(1).broadcast_to([P, out.shape[1], D]), ALU.add)

            def x_bias(j, u):
                hold(net, gp, x_in[u], j * 16 + 16)
                bias(XB[u][:], X[u][:], net.c12).then_inc(x_biased[u], 1)

            def scales(j, u):
                hold(net, gp, var1[u], j + 1)
                G_.tensor_tensor(S[u][:, 72:80], S[u][:, 64:72], net.neg_half[:, 0:8], ALU.pow).then_inc(scaled[u], 1)

            def x2_bias(j, u):
                for h in range(2):
                    hold(net, gp, x2_ready[u], j * G + (2 * h + 2))
                    bias(B[u][:, 2 * h:2 * h + 2, :], Y[u][:, 2 * h:2 * h + 2, :], net.bc["beta"]).then_inc(x2_biased[u], 1)

            def dev_3(j, u):
                hold(net, gp, var3[u], j + 1)
                G_.tensor_tensor(S[u][:, 84:88], S[u][:, 80:84], net.neg_half[:, 0:4], ALU.pow).then_inc(dev3[u], 1)
                hold(net, gp, dev3[u], j + 1)
                G_.tensor_tensor(S[u][:, 116:120], S[u][:, 112:116], S[u][:, 84:88], ALU.mult).then_inc(shift3[u], 1)

            def x3_bias(j, u):
                for h in range(2):
                    hold(net, gp, x3_ready[u], j * G + (2 * h + 2))
                    bias(B[u][:, 2 * h:2 * h + 2, :], Y[u][:, 2 * h:2 * h + 2, :], net.bc["b_out"]).then_inc(x3_biased[u], 1)

            def dev_5(j, u):
                hold(net, gp, var5[u], j + 1)
                G_.tensor_tensor(S[u][:, 96:100], S[u][:, 88:92], net.neg_half[:, 0:4], ALU.pow).then_inc(dev5[u], 1)
                hold(net, gp, dev5[u], j + 1)
                G_.tensor_tensor(S[u][:, 100:104], S[u][:, 92:96], S[u][:, 96:100], ALU.mult).then_inc(shift5[u], 1)

            def store_rep(t, u, n):
                hold(net, gp, rep_stored[u], n * 16)
                G_.tensor_copy(slot[u][:, 0:1], col(net.rep_node, t)).then_inc(slot_ready[u], 1)
                G_.tensor_copy(slot[u][:, 1:2], col(net.pos_i, t)).then_inc(slot_ready[u], 1)
                hold(net, gp, slot_ready[u], n * 2 + 2)
                G_.indirect_dma_start(net.rep, bass.IndirectOffsetOnAxis(slot[u][:, 0:1], 0), slot[u][:, 1:2], None,
                                      bounds_check=N - 1, oob_is_err=False).then_inc(rep_stored[u], 16)

            def turn(j, u, n=2):
                if n >= 1:
                    x2_bias(*ahead(j, u, 1))
                if n >= 2:
                    x_bias(*ahead(j, u, 2))
                if n >= 1:
                    dev_3(*ahead(j, u, 1))
                x3_bias(j, u)
                if n >= 2:
                    scales(*ahead(j, u, 2))
                dev_5(j, u)
            x_bias(0, 0)
            scales(0, 0)
            x2_bias(0, 0)
            x_bias(0, 1)
            dev_3(0, 0)
            scales(0, 1)
            with gp.Fori(0, LAST) as j:
                for u in range(2):
                    turn(j, u)
                    store_rep(j * 2 + u, u, j)
            turn(LAST, 0, 1)
            turn(LAST, 1, 0)
            for t in range(2 * LAST, net.T):
                store_rep(t, t % 2, t // 2)
            for u in range(2):
                gp.wait_ge(rep_stored[u], 16 * (net.T // 2))

        @block.tensor
        def _(pe):
            def transposes(bank, src, u, h):
                for c in range(C):
                    for i in range(2):
                        mm = nc.tensor.transpose(bank[:, (2 * c + i) * P:(2 * c + i + 1) * P], src[u][:, 2 * h + i, c * P:(c + 1) * P], net.ident[:])
                return mm

            def xt(j, u, h):
                if h == 0:
                    pe.wait_ge(x_in[u], j * 16 + 16)
                pe.wait_ge(xt_moved, j * 4 + (2 * u + h))
                transposes(tps[0], X, u, h).then_inc(xt_made, 1)

            def x3t(j, u, h):
                pe.wait_ge(x3_ready[u], j * G + (2 * h + 2))
                pe.wait_ge(x3t_moved, j * 4 + (2 * u + h))
                transposes(tps[1], Y, u, h).then_inc(x3t_made, 1)

            def project(j, u, h):
                pe.wait_ge(xt_moved, j * 4 + (2 * u + h + 1))
                pe.wait_ge(y_ready[h], j * 2 + u)
                for i in range(2):
                    for c in range(C):
                        mm = nc.tensor.matmul(prs[h][:, i * D:(i + 1) * D], XT[h][:, c, i * P:(i + 1) * P], net.w12[:, c, :], start=c == 0, stop=c == C - 1)
                mm.then_inc(pr[h], 1)

            def hidden(j, u, h):
                pe.wait_ge(x3t_moved, j * 4 + (2 * u + h + 1))
                pe.wait_ge(silu[h], j * 2 + u)
                for m in range(C):
                    for c in range(C):
                        mm = nc.tensor.matmul(hds[h][:, 2 * m * P:2 * (m + 1) * P], net.w_in[:, c, m * P:(m + 1) * P], X3T[h][:, c, :],
                                              start=c == 0, stop=c == C - 1)
                mm.then_inc(hid[h], 1)

            def out_project(j, u, h):
                pe.wait_ge(silu[h], j * 2 + (u + 1))
                pe.wait_ge(y5[h], j * 2 + u)
                for i in range(2):
                    for m in range(C):
                        mm = nc.tensor.matmul(ops[h][:, i * D:(i + 1) * D], HT[h][:, m, i * P:(i + 1) * P], net.w_out[:, m, :], start=m == 0, stop=m == C - 1)
                mm.then_inc(outp[h], 1)

            def first(j, u):
                for h in range(2):
                    xt(j, u, h)
                    project(j, u, h)

            def last(j, u):
                for h in range(2):
                    x3t(j, u, h)
                for h in range(2):
                    hidden(j, u, h)
                for h in range(2):
                    out_project(j, u, h)
            first(0, 0)
            first(0, 1)
            with pe.Fori(0, LAST) as j:
                for u in range(2):
                    first(*ahead(j, u, 2))
                    last(j, u)
            last(LAST, 0)
            last(LAST, 1)

        @block.scalar
        def _(act):
            def move_x(j, u, h):
                act.wait_ge(xt_made, j * 4 + (2 * u + h + 1))
                act.wait_ge(pr[h], j * 2 + u)
                nc.scalar.activation(XT[h][:].rearrange("p c e -> p (c e)"), tps[0][:, :], ACT.Copy).then_inc(xt_moved, 1)

            def move_x3(j, u, h):
                act.wait_ge(x3t_made, j * 4 + (2 * u + h + 1))
                act.wait_ge(hid[h], j * 2 + u)
                nc.scalar.activation(X3T[h][:].rearrange("p c e -> p (c e)"), tps[1][:, :], ACT.Copy).then_inc(x3t_moved, 1)

            def activate(j, u, h):
                act.wait_ge(hid[h], j * 2 + (u + 1))
                act.wait_ge(outp[h], j * 2 + u)
                for m in range(C):
                    mv = nc.scalar.activation(HT[h][:, m, :], hds[h][:, 2 * m * P:2 * (m + 1) * P], ACT.Silu, bias=net.cols[:, 2, m:m + 1])
                mv.then_inc(silu[h], 1)

            def norm_store(j, u):
                act.wait_ge(shift5[u], j + 1)
                act.wait_ge(stored[u], j * 16)
                for g in range(G):
                    nc.scalar.activation(O[u][:, g, :], W[u][:, g, :], ACT.Identity, bias=S[u][:, 100 + g:101 + g],
                                         scale=S[u][:, 96 + g:97 + g]).then_inc(o_ready[u], 1)
                act.wait_ge(o_ready[u], j * G + G)
                if isinstance(j, int) and j == LAST and u:
                    act.wait_ge(stored[0], 16 * (LAST + 1))
                act.dma_start(rows_of(a["out"], start_of(j, u)), O[u][:]).then_inc(stored[u], 16)

            def third_norm(j, u):
                act.wait_ge(shift3[u], j + 1)
                for g in range(G):
                    nc.scalar.activation(Y[u][:, g, :], Z[u][:, g, :], ACT.Identity, bias=S[u][:, 116 + g:117 + g],
                                         scale=S[u][:, 84 + g:85 + g]).then_inc(x3_ready[u], 1)

            def last(j, u):
                third_norm(j, u)
                for h in range(2):
                    move_x3(j, u, h)
                for h in range(2):
                    activate(j, u, h)

            def turn(j, u, n=3):
                if n >= 3:
                    for h in range(2):
                        move_x(*ahead(j, u, 3), h)
                if n >= 1:
                    last(*ahead(j, u, 1))
                norm_store(j, u)
            for b in range(3):
                for h in range(2):
                    move_x(*ahead(0, 0, b), h)
            last(0, 0)
            with act.Fori(0, LAST - 1) as j:
                for u in range(2):
                    turn(j, u)
            for n in (3, 2, 1, 0):
                turn(*ahead(LAST, 1, -n), n)
            for u in range(2):
                act.wait_ge(stored[u], 16 * (LAST + 1))

        @block.vector
        def _(dve):
            V = nc.vector

            def stats(ch, u, src, g):
                ch(V.bn_stats(S[u][:, 6 * g:6 * g + 6], src[u][:, g, :]))

            def aggregate(ch, u, at=24):
                hold(net, dve, ch.sem, ch.base + ch.k)
                for g in range(G):
                    ch(V.bn_aggr(S[u][:, at + 2 * g:at + 2 + 2 * g], S[u][:, 6 * g:6 * g + 6]))
                ch.wait()

            def first_norm(j, u):
                ch = Chain(dve, chain1[u], 11, j)
                for h in range(2):
                    dve.wait_ge(pr[h], j * 2 + (u + 1))
                    dve.wait_ge(x_biased[u], j + 1)
                    V.tensor_tensor(half(XB, u, h), prs[h][:, 0:2 * D], half(XB, u, h), ALU.add).then_inc(y_ready[h], 1)
                for g in range(G):
                    dve.wait_ge(y_ready[g // 2], j * 2 + (u + 1))
                    stats(ch, u, XB, g)
                aggregate(ch, u, 104)
                var = S[u][:, 105:112:2]
                ch(V.tensor_scalar(S[u][:, 64:68], var, 1 + EPS, EPS * EPS, ALU.mult, ALU.add))
                ch(V.tensor_scalar(S[u][:, 68:72], var, 1 + EPS * (1 + EPS), EPS ** 3, ALU.mult, ALU.add))
                ch.wait()
                ch(V.reciprocal(S[u][:, 60:64], S[u][:, 64:68]))
                ch.wait()
                V.tensor_tensor(S[u][:, 68:72], S[u][:, 68:72], S[u][:, 60:64], ALU.mult).then_inc(var1[u], 1)
                ch.close()

            def scale_shift(j, u):
                ch = Chain(dve, chain3[u], 15, j)
                dve.wait_ge(scaled[u], j + 1)
                for g in range(G):
                    V.tensor_scalar(Y[u][:, g, :], XB[u][:, g, :], S[u][:, 104 + 2 * g:105 + 2 * g], S[u][:, 72 + g:73 + g], ALU.subtract, ALU.mult).then_inc(x2_ready[u], 1)
                for g in range(G):
                    dve.wait_ge(x2_ready[u], j * G + (g + 1))
                    ch(V.scalar_tensor_tensor(Z[u][:, g, :], Y[u][:, g, :], S[u][:, 76 + g:77 + g], net.bc["gamma"][:], ALU.mult, ALU.mult))
                ch.wait()
                for h in range(2):
                    dve.wait_ge(x2_biased[u], j * 2 + (h + 1))
                    ch(V.tensor_tensor(half(Z, u, h), half(Z, u, h), half(B, u, h), ALU.add))
                ch.wait()
                for g in range(G):
                    stats(ch, u, Z, g)
                aggregate(ch, u)
                ch(V.tensor_scalar(S[u][:, 112:116], S[u][:, 24:32:2], -1.0, None, ALU.mult))
                V.tensor_scalar(S[u][:, 80:84], S[u][:, 25:32:2], EPS, None, ALU.add).then_inc(var3[u], 1)
                ch.close()

            def last_norm(j, u):
                ch = Chain(dve, chain6[u], 9, j)
                dve.wait_ge(o_ready[u], j * G)
                for h in range(2):
                    dve.wait_ge(outp[h], j * 2 + (u + 1))
                    dve.wait_ge(x3_biased[u], j * 2 + (h + 1))
                    V.tensor_tensor(half(W, u, h), ops[h][:, 0:2 * D], half(B, u, h), ALU.add).then_inc(y5[h], 1)
                for g in range(G):
                    dve.wait_ge(y5[g // 2], j * 2 + (u + 1))
                    stats(ch, u, W, g)
                aggregate(ch, u)
                ch(V.tensor_scalar(S[u][:, 92:96], S[u][:, 24:32:2], -1.0, None, ALU.mult))
                ch.wait()
                V.tensor_scalar(S[u][:, 88:92], S[u][:, 25:32:2], EPS, None, ALU.add).then_inc(var5[u], 1)
                ch.close()

            def turn(j, u, n=2):
                if n >= 1:
                    scale_shift(*ahead(j, u, 1))
                if n >= 2:
                    first_norm(*ahead(j, u, 2))
                last_norm(j, u)
            first_norm(0, 0)
            scale_shift(0, 0)
            first_norm(0, 1)
            with dve.Fori(0, LAST) as j:
                for u in range(2):
                    turn(j, u)
            turn(LAST, 0, 1)
            turn(LAST, 1, 0)


def load_store(eng, turns, n, load, store):
    for u in range(n):
        load(0, u)
    with eng.Fori(0, turns - 1) as j:
        for u in range(n):
            store(j, u)
            load(j + 1, u)
    for u in range(n):
        store(turns - 1, u)


def rows2(net, tab, t, i):
    return tab[bass.ds(t * P + i * net.R, P), :]


def keys_of(net, t):
    return net.a["key_out"][bass.ds(t, 1), :].broadcast_to([P, P])


def gather(net, out, table, index):
    return net.nc.gpsimd.indirect_dma_start(out, None, table, bass.IndirectOffsetOnAxis(index, 0))


def project1(net):
    nc, a, D, C, T, H = net.nc, net.a, net.D, net.C, net.T, net.H
    U, TURNS = 4, T // 4
    with Stage(nc) as st:
        X = st.sb("a_x", [P, 4, D], n=U)
        XT = st.sb("a_xt", [P, 4, P], n=2)
        I = st.sb("a_i", [P, 2], I32, n=U)
        RP = st.sb("a_rep", [P, 1], I32, n=U)
        idx, got, tp, xt, pr, hs, hd, spill = (st.sem(f"a_{n}", U) for n in (
            "index_ready", "gathered", "transposed", "xt_ready", "projected", "src_ready", "dst_ready", "spilled"))
        tps, hss, hds = (st.ps(f"a_ps_{n}", 2) for n in ("t", "s", "d"))
        block = st.ctx.enter_context(nc.Block())

        @block.sync
        def _(sp):
            with sp.Fori(0, TURNS) as j:
                for u in range(U):
                    sp.wait_ge(*upto(hs, u, j))
                    sp.wait_ge(*upto(hd, u, j))
                    sp.dma_start(tile_of(net.proj1, j * U + u), X[u][:].rearrange("p a d -> p (a d)")).then_inc(spill[u], 16)
            for u in range(U):
                sp.wait_ge(spill[u], 16 * TURNS)

        @block.gpsimd
        def _(gp):
            with gp.Fori(0, TURNS) as j:
                for u in range(U):
                    gp.wait_ge(*upto(hd, u, j, back=U))
                    hold(net, gp, *upto(spill, u, j, back=U, inc=16))
                    nc.gpsimd.tensor_copy(I[u][:], net.index[:, bass.ds(j * U + u, 1), :].rearrange("p o k -> p (o k)")).then_inc(idx[u], 1)
                    hold(net, gp, *upto(idx, u, j))
                    for i in range(2):
                        gather(net, X[u][:, i, :], a["x"], I[u][:, i:i + 1]).then_inc(got[u], 16)
                    gather(net, RP[u][:], net.rep, I[u][:, 0:1]).then_inc(got[u], 16)

        @block.tensor
        def _(pe):
            with pe.Fori(0, TURNS) as j:
                for u in range(U):
                    b = u % 2
                    pe.wait_ge(*upto(got, u, j, inc=48))
                    pe.wait_ge(*upto(xt, u, j, back=2))
                    for k in range(4):
                        mm = nc.tensor.transpose(tps[b][:, k * P:(k + 1) * P], X[u][:, k // 2, (k % 2) * P:(k % 2 + 1) * P], net.ident[:])
                    mm.then_inc(tp[u], 1)
                    pe.wait_ge(*upto(xt, u, j))
                    pe.wait_ge(*upto(hs, u, j, back=2))
                    pe.wait_ge(*upto(hd, u, j, back=2))
                    for c in range(C):
                        nc.tensor.matmul(hds[b][:, 0:D + 2 * H], XT[b][:, 2 + c, :], net.w1x[:, c, 0:D + 2 * H], start=c == 0, stop=False, skip_group_check=True)
                    for c in range(C):
                        nc.tensor.matmul(hds[b][:, D:D + H], XT[b][:, c, :], net.w1x[:, c, D + 2 * H:D + 3 * H], start=False, stop=c == C - 1, skip_group_check=True)
                    for c in range(C):
                        mm = nc.tensor.matmul(hss[b][:, 0:D], XT[b][:, c, :], net.w1x[:, c, 0:D], start=c == 0, stop=c == C - 1)
                    mm.then_inc(pr[u], 1)

        @block.scalar
        def _(act):
            with act.Fori(0, TURNS) as j:
                for u in range(U):
                    act.wait_ge(*upto(tp, u, j))
                    act.wait_ge(*upto(pr, u, j, back=2))
                    nc.scalar.activation(XT[u % 2][:].rearrange("p k e -> p (k e)"), tps[u % 2][:, :], ACT.Copy).then_inc(xt[u], 1)
                    act.wait_ge(*upto(pr, u, j))
                    nc.scalar.activation(X[u][:, 2, :], hss[u % 2][:, 0:D], ACT.Copy).then_inc(hs[u], 1)

        @block.vector
        def _(dve):
            V = nc.vector
            with dve.Fori(0, TURNS) as j:
                for u in range(U):
                    t = j * U + u
                    dve.wait_ge(*upto(pr, u, j))
                    V.tensor_copy(X[u][:, 3, :], hds[u % 2][:, 0:D])
                    V.tensor_copy(net.scores[:, :, bass.ds(t, 1)], hds[u % 2][:, D:D + 2 * H].unsqueeze(2))
                    V.tensor_copy(col(net.src_rep, t), RP[u][:]).then_inc(hd[u], 1)


def softmax(net, layer):
    nc, T, H = net.nc, net.T, net.H
    n = 1 if layer == 2 else H
    own = layer != 3
    m = n * P
    with Stage(nc) as st:
        L = st.sb("sm_logits", [T, H * P])
        S = st.sb("sm_own", [T, H * P])
        W = st.sb("sm_work", [T, H * P])
        dots = st.sb("sm_dots", [T, 3 * P])
        is_dst = st.sb("sm_is_dst", [P, T])
        tmp = st.sb("sm_tmp", [P, T])
        seg = Segments(net, st)
        bank = st.ps("sm_bank", 4)
        rows_ready, rows_moved, exp_ask, exp_done, w_ready, cols_ready, chain = (st.sem(f"sm_{x}") for x in (
            "rows_ready", "rows_moved", "exp_ask", "exp_done", "weights_ready", "cols_ready", "dve_chain"))
        srcs = [(L, h) for h in range(n)] + ([(S, h) for h in range(n)] if own else [])
        block = st.ctx.enter_context(nc.Block())

        @block.tensor
        def _(pe):
            if layer == 2:
                for k in range(3):
                    mm = nc.tensor.transpose(bank[0][0:T, k * P:(k + 1) * P], net.dots2[:, k, :], net.ident[:])
                mm.then_inc(rows_ready, 1)
                seg.cross_pe(pe, 2, False)
            else:
                k_all = 2 * H if own else H
                for b in range(k_all // 4):
                    for k in range(4):
                        mm = nc.tensor.transpose(bank[b][0:T, k * P:(k + 1) * P], net.scores[:, 4 * b + k, :], net.ident[:])
                    mm.then_inc(rows_ready, 1)
            seg.cross_pe(pe, n, True)
            seg.cross_pe(pe, n, False)
            pe.wait_ge(w_ready, 1)
            for b in range(-(-len(srcs) // 4)):
                for i, (buf, h) in enumerate(srcs[4 * b:4 * b + 4]):
                    mm = nc.tensor.transpose(bank[b][:, i * T:(i + 1) * T], buf[:, h * P:(h + 1) * P], net.ident[0:T, 0:T])
                mm.then_inc(cols_ready, 1)

        @block.scalar
        def _(act):
            if layer == 2:
                act.wait_ge(rows_ready, 1)
                nc.scalar.activation(dots[:], bank[0][0:T, 0:3 * P], ACT.Copy).then_inc(rows_moved, 1)
            else:
                for b in range((2 * H if own else H) // 4):
                    act.wait_ge(rows_ready, b + 1)
                    dst = L if b < 2 else S
                    nc.scalar.activation(dst[:, (b % 2) * 4 * P:(b % 2 + 1) * 4 * P], bank[b][0:T, :], ACT.Copy).then_inc(rows_moved, 1)
            act.wait_ge(exp_ask, 1)
            if own:
                nc.scalar.activation(S[:, 0:m], S[:, 0:m], ACT.Exp)
            nc.scalar.activation(L[:, 0:m], L[:, 0:m], ACT.Exp).then_inc(exp_done, 1)
            for b in range(-(-len(srcs) // 4)):
                act.wait_ge(cols_ready, b + 1)
                w = min(4, len(srcs) - 4 * b)
                nc.scalar.activation(net.scores[:, 4 * b:4 * b + w, :].rearrange("p k t -> p (k t)"), bank[b][:, 0:w * T], ACT.Copy)

        @block.vector
        def _(dve):
            V = nc.vector
            ch = Chain(dve, chain)
            if layer == 1:
                ch(V.tensor_scalar(is_dst[:], net.src_rep[:], 0.0, None, ALU.is_ge))
                ch(V.tensor_scalar(tmp[:], net.pos[:], float(net.R), None, ALU.add))
                ch.wait()
                ch(V.tensor_tensor(net.src_rep[:], net.src_rep[:], tmp[:], ALU.subtract))
                ch.wait()
                ch(V.tensor_tensor(net.src_rep[:], net.src_rep[:], is_dst[:], ALU.mult))
                ch.wait()
                ch(V.tensor_tensor(net.src_rep[:], net.src_rep[:], tmp[:], ALU.add))
                ch.wait()
                ch(V.tensor_copy(net.table_row[:], net.src_rep[:]))
                ch(V.tensor_scalar(net.term_row[:], net.src_rep[:], float(net.R), None, ALU.min))
            if layer == 2:
                dve.wait_ge(rows_moved, 1)
                for k in (1, 2):
                    ch(V.tensor_tensor(dots[:, k * P:(k + 1) * P], dots[:, k * P:(k + 1) * P], net.is_rep[:], ALU.mult))
                seg.sum_dve(ch, W, dots[:, P:3 * P], 2)
                ch.wait()
                ch(V.tensor_tensor(L[:, 0:P], dots[:, 0:P], W[:, 0:P], ALU.add))
                ch(V.tensor_tensor(S[:, 0:P], W[:, 0:P], W[:, P:2 * P], ALU.add))
            else:
                dve.wait_ge(rows_moved, (2 * H if own else H) // 4)
            for buf in (L, S) if own else (L,):
                ch.wait()
                if own:
                    ch(V.scalar_tensor_tensor(buf[:, 0:m], buf[:, 0:m], 0.2, buf[:, 0:m], ALU.mult, ALU.max))
                else:
                    ch(V.tensor_scalar(buf[:, 0:m], buf[:, 0:m], float(net.D // H) ** -0.5, None, ALU.mult))
            ch.wait()
            ch(V.memset(heads(L[:, 0:m], n)[:, :, 0:1], -BIG))
            seg.max_dve(ch, W, L, n)
            ch.wait()
            if own:
                ch(V.tensor_tensor(W[:, 0:m], W[:, 0:m], S[:, 0:m], ALU.max))
                ch.wait()
                ch(V.tensor_tensor(S[:, 0:m], S[:, 0:m], W[:, 0:m], ALU.subtract))
            ch(V.tensor_tensor(L[:, 0:m], L[:, 0:m], W[:, 0:m], ALU.subtract))
            ch.wait()
            dve.sem_inc(exp_ask, 1)
            dve.wait_ge(exp_done, 1)
            ch(V.memset(heads(L[:, 0:m], n)[:, :, 0:1], 0.0))
            seg.sum_dve(ch, W, L, n)
            ch.wait()
            if own:
                ch(V.tensor_tensor(W[:, 0:m], W[:, 0:m], S[:, 0:m], ALU.add))
                ch.wait()
                ch(V.tensor_scalar(W[:, 0:m], W[:, 0:m], 1e-16, None, ALU.add))
            else:
                ch(V.tensor_scalar(W[:, 0:m], W[:, 0:m], 1e-16, None, ALU.max))
            ch.wait()
            ch(V.reciprocal(W[:, 0:m], W[:, 0:m]))
            ch.wait()
            ch(V.tensor_tensor(L[:, 0:m], L[:, 0:m], W[:, 0:m], ALU.mult))
            if own:
                ch(V.tensor_tensor(S[:, 0:m], S[:, 0:m], W[:, 0:m], ALU.mult))
            ch.wait()
            dve.sem_inc(w_ready, 1)


class Tiles:

    def __init__(self, net, st, n, apart=False):
        self.net, self.n, self.w = net, n, net.D // 2
        self.keys = st.sb("keys_out", [P, P], I32, n=n)
        self.eq = st.sb("equal", [P, P], n=n)
        self.msg = st.sb("messages", [P, net.D], n=n)
        if apart:
            self.banks = [st.ps(f"sum_bank_{s}_", n) for s in range(2)]
        else:
            assert n * self.w <= 512
            self.pair = st.ctx.enter_context(net.nc.psum_tensor(st.tag + "sum_banks", [P, 2, 512], F32))
        self.apart = apart
        self.summed = [st.sem(f"summed_{s}_", n) for s in range(2)]
        self.msg_ready = [st.sem(f"msg_ready_{s}_", n) for s in range(2)]
        self.eq_ready = st.sem("eq_ready", n)
        self.first_carry = st.sem("first_carry")

    def half(self, s, u, rows=P):
        if self.apart:
            return self.banks[s][u][0:rows, 0:self.w]
        return self.pair[0:rows, s, u * self.w:(u + 1) * self.w]

    def total(self, u):
        return self.pair[:, :, u * self.w:(u + 1) * self.w]

    def halves(self, ap):
        return ap.rearrange("p (s w) -> p s w", s=2)

    def start(self, dve):
        for s in range(2):
            self.net.nc.vector.memset(self.half(s, self.n - 1, 1), 0.0).then_inc(self.first_carry, 1)
        dve.wait_ge(self.first_carry, 2)

    def equal(self, dve, u, j):
        net = self.net
        dve.wait_ge(*upto(self.summed[1], u, j, back=self.n))
        return net.nc.vector.tensor_scalar(self.eq[u][:], self.keys[u][:], col(net.key_in, j * self.n + u), None, ALU.is_equal)

    def carry(self, dve, u, j):
        for s in range(2):
            dve.wait_ge(*upto(self.summed[s], u, j, back=1))
            self.net.nc.vector.tensor_copy(self.msg[u][0:1, s * self.w:(s + 1) * self.w],
                                           self.half(s, (u - 1) % self.n, 1)).then_inc(self.msg_ready[s][u], 1)

    def sum_pe(self, pe, u, j):
        for s in range(2):
            pe.wait_ge(*upto(self.msg_ready[s], u, j))
            self.net.nc.tensor.matmul(self.half(s, u), self.eq[u][:], self.msg[u][:, s * self.w:(s + 1) * self.w],
                                      start=True, stop=True).then_inc(self.summed[s][u], 1)


def following(n, j, u):
    return (j, u + 1) if u + 1 < n else (j + 1, 0)


def turns_ahead(eng, turns, first, turn):
    first(0)
    with eng.Fori(0, turns - 1) as j:
        turn(j, True)
    turn(turns - 1, False)


def weighted(net, out, x, k, n, t):
    return net.nc.vector.tensor_tensor(heads(out, n), heads(x, n),
                                       net.scores[:, k:k + n, bass.ds(t, 1)].broadcast_to([P, n, net.D // n]), ALU.mult)


def gat1(net):
    nc, a, D, T, H = net.nc, net.a, net.D, net.T, net.H
    U, TURNS = 4, T // 4
    with Stage(nc) as st:
        ti = Tiles(net, st, n=U)
        X = st.sb("b_x", [P, 2, D], n=U)
        A = st.sb("b_own", [P, D], n=U)
        O = st.sb("b_out", [P, 2, D], n=U)
        J = st.sb("b_junk", [P, 2, D], n=U)
        d2 = st.sb("b_dots", [P, 2], n=U)
        x_in, k_in, wx, aux, aux2, o_dst, o_src, dots, done, stored = (st.sem(f"b_{n}", U) for n in (
            "x_loaded", "keys_loaded", "weighted", "own_weighted", "own_biased", "out_dst_ready", "out_src_ready", "dots_ready", "tile_done", "stored"))
        block = st.ctx.enter_context(nc.Block())

        @block.sync
        def _(sp):
            def load(j, u):
                sp.wait_ge(*upto(aux, u, j, back=U))
                sp.wait_ge(*upto(o_src, u, j, back=U))
                sp.dma_start(X[u][:].rearrange("p a d -> p (a d)"), net.proj1[bass.ds(j * U + u, 1), :, 2 * D:4 * D].rearrange("o p d -> (o p) d")).then_inc(x_in[u], 16)
                sp.dma_start(ti.keys[u][:], keys_of(net, j * U + u)).then_inc(k_in[u], 16)

            with sp.Fori(0, TURNS) as j:
                for u in range(U):
                    load(j, u)

        @block.scalar
        def _(act):
            with act.Fori(0, TURNS) as j:
                for i, ready in ((1, o_src), (0, o_dst)):
                    for u in range(U):
                        act.wait_ge(*upto(ready, u, j))
                        act.dma_start(rows2(net, net.out1, j * U + u, i), O[u][:, i, :]).then_inc(stored[u], 16)
            for u in range(U):
                act.wait_ge(stored[u], 32 * TURNS)

        @block.gpsimd
        def _(gp):
            with gp.Fori(0, TURNS) as j:
                for u in range(U):
                    gp.wait_ge(*upto(x_in, u, j, inc=16))
                    hold(net, gp, *upto(stored, u, j, back=U, inc=32))
                    nc.gpsimd.tensor_tensor(O[u][:, 1, :], X[u][:, 0, :], net.bc["b1"][:], ALU.add).then_inc(o_src[u], 1)
                for u in range(U):
                    hold(net, gp, *upto(aux, u, j))
                    nc.gpsimd.tensor_tensor(A[u][:], A[u][:], net.bc["b1"][:], ALU.add).then_inc(aux2[u], 1)

        @block.tensor
        def _(pe):
            with pe.Fori(0, TURNS) as j:
                for u in range(U):
                    ti.sum_pe(pe, u, j)

        @block.vector
        def _(dve):
            V = nc.vector
            ti.start(dve)

            def messages(j):
                for u in range(U):
                    t = j * U + u
                    dve.wait_ge(*upto(k_in, u, j, inc=16))
                    ti.equal(dve, u, j)
                    dve.wait_ge(*upto(x_in, u, j, inc=16))
                    weighted(net, ti.msg[u][:], X[u][:, 0, :], 0, H, t).then_inc(wx[u], 1)
                    dve.wait_ge(*upto(o_dst, u, j, back=U))
                    weighted(net, A[u][:], X[u][:, 1, :], H, H, t).then_inc(aux[u], 1)
                    dve.wait_ge(*upto(wx, u, j))
                    ti.carry(dve, u, j)

            def turn(j, more):
                dve.wait_ge(*upto(ti.summed[1], U - 1, j))
                for u in range(U):
                    dve.wait_ge(*upto(aux2, u, j))
                    dve.wait_ge(*upto(stored, u, j, back=U, inc=32))
                    V.tensor_tensor(ti.halves(O[u][:, 0, :]), ti.total(u), ti.halves(A[u][:]), ALU.add).then_inc(o_dst[u], 1)
                if more:
                    messages(j + 1)
                for u in range(U):
                    t = j * U + u
                    dve.wait_ge(*upto(o_dst, u, j))
                    for k in range(2):
                        V.tensor_tensor_reduce(J[u][:, k, :], O[u][:, 0, :], net.att2[:, 1 - k, :], 1.0, 0.0, ALU.mult, ALU.add,
                                               d2[u][:, k:k + 1]).then_inc(dots[u], 1)
                    dve.wait_ge(*upto(dots, u, j, inc=2))
                    V.tensor_copy(net.dots2[:, 1:3, bass.ds(t, 1)], d2[u][:].unsqueeze(2)).then_inc(done[u], 1)
            turns_ahead(dve, TURNS, messages, turn)


def gather_out1(net):
    nc, D, T = net.nc, net.D, net.T
    U, TURNS = 4, T // 4
    with Stage(nc) as st:
        X = st.sb("c_x", [P, D], n=U)
        J = st.sb("c_junk", [P, D], n=U)
        d1 = st.sb("c_dot", [P, 1], n=U)
        I = st.sb("c_i", [P, 1], I32, n=U)
        idx, got, dot, done, spill = (st.sem(f"c_{n}", U) for n in ("index_ready", "gathered", "dot_ready", "tile_done", "spilled"))
        block = st.ctx.enter_context(nc.Block())

        @block.sync
        def _(sp):
            with sp.Fori(0, TURNS) as j:
                for u in range(U):
                    sp.wait_ge(*upto(got, u, j, inc=16))
                    sp.dma_start(tile_of(net.out1_src, j * U + u), X[u][:]).then_inc(spill[u], 16)
            for u in range(U):
                sp.wait_ge(spill[u], 16 * TURNS)

        @block.gpsimd
        def _(gp):
            with gp.Fori(0, TURNS) as j:
                for u in range(U):
                    gp.wait_ge(*upto(done, u, j, back=U))
                    hold(net, gp, *upto(spill, u, j, back=U, inc=16))
                    nc.gpsimd.tensor_copy(I[u][:], col(net.table_row, j * U + u)).then_inc(idx[u], 1)
                    hold(net, gp, *upto(idx, u, j))
                    gather(net, X[u][:], net.out1, I[u][:]).then_inc(got[u], 16)

        @block.vector
        def _(dve):
            with dve.Fori(0, TURNS) as j:
                for u in range(U):
                    dve.wait_ge(*upto(got, u, j, inc=16))
                    dve.wait_ge(*upto(done, u, j, back=U))
                    nc.vector.tensor_tensor_reduce(J[u][:], X[u][:], net.att2[:, 0, :], 1.0, 0.0, ALU.mult, ALU.add, d1[u][:]).then_inc(dot[u], 1)
                    dve.wait_ge(*upto(dot, u, j))
                    nc.vector.tensor_copy(net.dots2[:, 0, bass.ds(j * U + u, 1)], d1[u][:]).then_inc(done[u], 1)


def gat2(net):
    nc, D, C, T = net.nc, net.D, net.C, net.T
    U, TURNS = 4, T // 4
    with Stage(nc) as st:
        ti = Tiles(net, st, n=U)
        XS = st.sb("d_src", [P, D], n=U)
        X = st.sb("d_x", [P, 2, D], n=U)
        O = st.sb("d_out1", [P, 2, D], n=U)
        A = st.sb("d_agg", [P, D], n=U)
        XT = st.sb("d_xt", [P, 4, P], n=U)
        Y = st.sb("d_y", [P, 2, D], n=U)
        S = st.sb("d_small", [P, 64], n=U)
        x_in, xb, wx, agg, tp, xt, pr, y_ready, var, dev, x1_ready, stored, chain = (st.sem(f"d_{n}", U) for n in (
            "loaded", "x_biased", "weighted", "agg_ready", "transposed", "xt_ready", "projected", "y_ready", "var_ready", "dev_ready",
            "x1_ready", "stored", "dve_chain"))
        tps, prs = (st.ps(f"d_ps_{n}", 2) for n in ("t", "p"))
        shift = st.sem("d_shift_ready", U)
        m_in = st.sem("d_messages_loaded", U)
        block = st.ctx.enter_context(nc.Block())

        @block.sync
        def _(sp):
            def load(j, u):
                t = j * U + u
                hold(net, sp, *upto(ti.summed[1], u, j, back=U))
                sp.dma_start(XS[u][:], tile_of(net.out1_src, t)).then_inc(m_in[u], 16)
                sp.dma_start(ti.keys[u][:], keys_of(net, t)).then_inc(m_in[u], 16)

            def load_x(j, u):
                t = j * U + u
                hold(net, sp, *upto(y_ready, u, j, back=U, inc=2))
                sp.dma_start(X[u][:].rearrange("p a d -> p (a d)"), net.proj1[bass.ds(t, 1), :, 0:2 * D].rearrange("o p d -> (o p) d")).then_inc(x_in[u], 16)
                for i in range(2):
                    sp.dma_start(O[u][:, i, :], rows2(net, net.out1, t, i)).then_inc(x_in[u], 16)

            with sp.Fori(0, TURNS) as j:
                for part in (load, load_x):
                    for u in range(U):
                        part(j, u)

        @block.gpsimd
        def _(gp):
            with gp.Fori(0, TURNS) as j:
                for u in range(U):
                    hold(net, gp, *upto(x_in, u, j, inc=48))
                    for i in range(2):
                        nc.gpsimd.tensor_tensor(X[u][:, i, :], X[u][:, i, :], net.bc["b2"][:], ALU.add).then_inc(xb[u], 1)
                for u in range(U):
                    hold(net, gp, *upto(var, u, j))
                    dev_shift(net, gp, S[u], 2, dev[u], shift[u], upto(dev, u, j)[1])

        @block.tensor
        def _(pe):
            def sums(j):
                for u in range(U):
                    ti.sum_pe(pe, u, j)

            def turn(j, more):
                for u in range(U):
                    transposes(j, u)
                    if u:
                        project(j, u - 1)
                project(j, U - 1)
                if more:
                    sums(j + 1)

            def transposes(j, u):
                pe.wait_ge(*upto(x_in, u, j, inc=48))
                pe.wait_ge(*upto(agg, u, j))
                pe.wait_ge(*upto(xt, u, j, back=2))
                for k in range(4):
                    src = A[u] if k < 2 else O[u][:, 1, :]
                    mm = nc.tensor.transpose(tps[u % 2][:, k * P:(k + 1) * P], src[:, (k % 2) * P:(k % 2 + 1) * P], net.ident[:])
                mm.then_inc(tp[u], 1)

            def project(j, u):
                pe.wait_ge(*upto(xt, u, j))
                pe.wait_ge(*upto(y_ready, u, j, back=2, inc=2))
                for i in range(2):
                    for c in range(C):
                        mm = nc.tensor.matmul(prs[u % 2][:, i * D:(i + 1) * D], XT[u][:, 2 * i + c, :], net.w2[:, c, :], start=c == 0, stop=c == C - 1)
                mm.then_inc(pr[u], 1)
            turns_ahead(pe, TURNS, sums, turn)

        @block.scalar
        def _(act):
            with act.Fori(0, TURNS) as j:
                for u in range(U):
                    act.wait_ge(*upto(tp, u, j))
                    act.wait_ge(*upto(pr, u, j, back=U))
                    nc.scalar.activation(XT[u][:].rearrange("p k e -> p (k e)"), tps[u % 2][:, :], ACT.Copy).then_inc(xt[u], 1)
                for u in range(U):
                    act.wait_ge(*upto(shift, u, j))
                    for i in range(2):
                        normed_act(net, Y[u][:, i, :], Y[u][:, i, :], S[u], i).then_inc(x1_ready[u], 1)
                    act.wait_ge(*upto(x1_ready, u, j, inc=2))
                    for i in range(2):
                        act.dma_start(rows2(net, net.x1, j * U + u, i), Y[u][:, i, :]).then_inc(stored[u], 16)
            for u in range(U):
                act.wait_ge(stored[u], 32 * TURNS)

        @block.vector
        def _(dve):
            V = nc.vector
            ti.start(dve)

            def messages(j):
                for u in range(U):
                    t = j * U + u
                    dve.wait_ge(*upto(m_in, u, j, inc=32))
                    ti.equal(dve, u, j)
                    weighted(net, ti.msg[u][:], XS[u][:], 0, 1, t).then_inc(wx[u], 1)
                    dve.wait_ge(*upto(wx, u, j))
                    ti.carry(dve, u, j)

            def turn(j, more):
                dve.wait_ge(*upto(ti.summed[1], U - 1, j))
                for u in range(U):
                    dve.wait_ge(*upto(x_in, u, j, inc=48))
                    dve.wait_ge(*upto(tp, u, j, back=U))
                    t = j * U + u
                    V.scalar_tensor_tensor(ti.halves(A[u][:]), ti.halves(O[u][:, 0, :]), net.scores[:, 1, bass.ds(t, 1)], ti.total(u), ALU.mult, ALU.add).then_inc(agg[u], 1)
                for u in range(U):
                    dve.wait_ge(*upto(pr, u, j))
                    dve.wait_ge(*upto(xb, u, j, inc=2))
                    dve.wait_ge(*upto(stored, u, j, back=U, inc=32))
                    for i in range(2):
                        V.tensor_tensor(Y[u][:, i, :], prs[u % 2][:, i * D:(i + 1) * D], X[u][:, 1 - i, :], ALU.add).then_inc(y_ready[u], 1)
                    ln_stats(net, dve, chain, j, S, lambda u: dve.wait_ge(*upto(y_ready, u, j, inc=2)),
                             lambda u: [Y[u][:, i, :] for i in range(2)], var, slots=[u])
                if more:
                    messages(j + 1)
            turns_ahead(dve, TURNS, messages, turn)


def project_qkv(net):
    nc, D, C, T, H = net.nc, net.D, net.C, net.T, net.H
    U, TURNS = 4, T // 4
    with Stage(nc) as st:
        X = st.sb("e_x", [P, 2, D], n=U)
        I = st.sb("e_i", [P, 2], I32, n=U)
        XT = st.sb("e_xt", [P, 4, P], n=2)
        KV = st.sb("e_k", [P, D], n=2)
        QK = st.sb("e_qk", [P, D], n=2)
        QV = st.sb("e_qv", [P, 2, D], n=2)
        bias = st.sb("e_bias", [P, 3, D])
        bias_in = st.sem("e_bias_loaded")
        biased = st.sem("e_biased", U)
        idx, got, tp, xt, pr, kv, qk, sc, stored = (st.sem(f"e_{n}", U) for n in (
            "index_ready", "gathered", "transposed", "xt_ready", "projected", "kv_ready", "product_ready", "scored", "stored"))
        tps, qvs, kps = (st.ps(f"e_ps_{n}", 2) for n in ("t", "qv", "k"))
        block = st.ctx.enter_context(nc.Block())

        @block.sync
        def _(sp):
            for k, name in enumerate(("bq", "bv", "bk")):
                sp.dma_start(bias[:, k, :], net.a[name].partition_broadcast(P)).then_inc(bias_in, 16)
            with sp.Fori(0, TURNS) as j:
                for u in range(U):
                    sp.wait_ge(*upto(biased, u, j, inc=2))
                    sp.dma_start(tile_of(net.v_edge, j * U + u), QV[u % 2][:, 1, :]).then_inc(stored[u], 16)
            for u in range(U):
                sp.wait_ge(stored[u], 16 * TURNS)

        @block.gpsimd
        def _(gp):
            with gp.Fori(0, TURNS) as j:
                for u in range(U):
                    hold(net, gp, *upto(tp, u, j, back=U))
                    nc.gpsimd.tensor_copy(I[u][:, 0:1], col(net.table_row, j * U + u)).then_inc(idx[u], 1)
                    nc.gpsimd.tensor_copy(I[u][:, 1:2], col(net.dst_row, j * U + u)).then_inc(idx[u], 1)
                    hold(net, gp, *upto(idx, u, j, inc=2))
                    for i in range(2):
                        gather(net, X[u][:, i, :], net.x1, I[u][:, i:i + 1]).then_inc(got[u], 16)

        @block.tensor
        def _(pe):
            def transposes(j, u):
                b = u % 2
                pe.wait_ge(*upto(got, u, j, inc=32))
                pe.wait_ge(*upto(xt, u, j, back=2))
                for k in range(4):
                    mm = nc.tensor.transpose(tps[b][:, k * P:(k + 1) * P], X[u][:, k // 2, (k % 2) * P:(k % 2 + 1) * P], net.ident[:])
                mm.then_inc(tp[u], 1)

            def project(j, u):
                b = u % 2
                pe.wait_ge(*upto(xt, u, j))
                pe.wait_ge(*upto(kv, u, j, back=2))
                pe.wait_ge(*upto(biased, u, j, back=2, inc=2))
                for c in range(C):
                    nc.tensor.matmul(qvs[b][:, :], XT[b][:, c, :], net.w_qv[:, c, :], start=c == 0, stop=c == C - 1)
                for c in range(C):
                    mm = nc.tensor.matmul(kps[b][:, 0:D], XT[b][:, 2 + c, :], net.w_k[:, c, :], start=c == 0, stop=c == C - 1)
                mm.then_inc(pr[u], 1)

            def turn(j, more):
                for u in range(U):
                    if more or u + 1 < U:
                        transposes(*following(U, j, u))
                    project(j, u)
            turns_ahead(pe, TURNS, lambda j: transposes(j, 0), turn)

        @block.scalar
        def _(act):
            def move(j, u):
                b = u % 2
                act.wait_ge(*upto(tp, u, j))
                act.wait_ge(*upto(pr, u, j, back=2))
                nc.scalar.activation(XT[b][:].rearrange("p k e -> p (k e)"), tps[b][:, :], ACT.Copy).then_inc(xt[u], 1)

            def keys_values(j, u):
                b = u % 2
                act.wait_ge(*upto(pr, u, j))
                act.wait_ge(*upto(qk, u, j, back=2))
                nc.scalar.activation(KV[b][:], kps[b][:, 0:D], ACT.Copy).then_inc(kv[u], 1)

            def turn(j, more):
                for u in range(U):
                    if more or u + 1 < U:
                        move(*following(U, j, u))
                    keys_values(j, u)
            turns_ahead(act, TURNS, lambda j: move(j, 0), turn)

        @block.vector
        def _(dve):
            V = nc.vector
            dve.wait_ge(bias_in, 48)
            with dve.Fori(0, TURNS) as j:
                for u in range(U):
                    b = u % 2
                    dve.wait_ge(*upto(pr, u, j))
                    dve.wait_ge(*upto(stored, u, j, back=2, inc=16))
                    dve.wait_ge(*upto(qk, u, j, back=2))
                    V.tensor_tensor(QV[b][:].rearrange("p a d -> p (a d)"), qvs[b][:, :],
                                    bias[:, 0:2, :].rearrange("p a d -> p (a d)"), ALU.add).then_inc(biased[u], 1)
                    dve.wait_ge(*upto(kv, u, j))
                    V.tensor_tensor(KV[b][:], KV[b][:], bias[:, 2, :], ALU.add).then_inc(biased[u], 1)
                    dve.wait_ge(*upto(biased, u, j, inc=2))
                    dve.wait_ge(*upto(sc, u, j, back=2))
                    V.tensor_tensor(QK[b][:], QV[b][:, 0, :], KV[b][:], ALU.mult).then_inc(qk[u], 1)
                    dve.wait_ge(*upto(qk, u, j))
                    V.tensor_reduce(net.scores[:, 0:H, bass.ds(j * U + u, 1)].rearrange("p h o -> p (h o)"), heads(QK[b][:], H), AXX, ALU.add).then_inc(sc[u], 1)


def attend(net):
    nc, D, T, H = net.nc, net.D, net.T, net.H
    U, TURNS = 4, T // 4
    with Stage(nc) as st:
        ti = Tiles(net, st, n=U)
        VE = st.sb("f_v", [P, D], n=U)
        X = st.sb("f_x", [P, 2, D], n=U)
        Y = st.sb("f_y", [P, D], n=U)
        O = st.sb("f_o", [P, 2, D], n=U)
        S = st.sb("f_small", [P, 64], n=U)
        x_in, wx, y_ready, var, dev, x2_ready, stored, chain = (st.sem(f"f_{n}", U) for n in (
            "loaded", "weighted", "y_ready", "var_ready", "dev_ready", "x2_ready", "stored", "dve_chain"))
        shift = st.sem("f_shift_ready", U)
        m_in = st.sem("f_messages_loaded", U)
        block = st.ctx.enter_context(nc.Block())

        @block.sync
        def _(sp):
            def load(j, u):
                t = j * U + u
                hold(net, sp, *upto(ti.summed[1], u, j, back=U))
                sp.dma_start(VE[u][:], tile_of(net.v_edge, t)).then_inc(m_in[u], 16)
                sp.dma_start(ti.keys[u][:], keys_of(net, t)).then_inc(m_in[u], 16)

            def load_x(j, u):
                t = j * U + u
                hold(net, sp, *upto(x2_ready, u, j, back=U, inc=2))
                for i in range(2):
                    sp.dma_start(X[u][:, i, :], rows2(net, net.x1, t, i)).then_inc(x_in[u], 16)

            with sp.Fori(0, TURNS) as j:
                for part in (load, load_x):
                    for u in range(U):
                        part(j, u)

        @block.scalar
        def _(act):
            with act.Fori(0, TURNS) as j:
                for u in range(U):
                    act.wait_ge(*upto(shift, u, j))
                    act.wait_ge(*upto(stored, u, j, back=U, inc=32))
                    normed_act(net, O[u][:, 0, :], Y[u][:], S[u], 0).then_inc(x2_ready[u], 1)
                    normed_act(net, O[u][:, 1, :], X[u][:, 1, :], S[u], 1).then_inc(x2_ready[u], 1)
                    act.wait_ge(*upto(x2_ready, u, j, inc=2))
                    for i in range(2):
                        act.dma_start(rows2(net, net.x2, j * U + u, i), O[u][:, i, :]).then_inc(stored[u], 16)
            for u in range(U):
                act.wait_ge(stored[u], 32 * TURNS)

        @block.gpsimd
        def _(gp):
            with gp.Fori(0, TURNS) as j:
                for u in range(U):
                    hold(net, gp, *upto(var, u, j))
                    dev_shift(net, gp, S[u], 2, dev[u], shift[u], upto(dev, u, j)[1])

        @block.tensor
        def _(pe):
            with pe.Fori(0, TURNS) as j:
                for u in range(U):
                    ti.sum_pe(pe, u, j)

        @block.vector
        def _(dve):
            V = nc.vector
            ti.start(dve)

            def messages(j):
                for u in range(U):
                    dve.wait_ge(*upto(m_in, u, j, inc=32))
                    ti.equal(dve, u, j)
                    weighted(net, ti.msg[u][:], VE[u][:], 0, H, j * U + u).then_inc(wx[u], 1)
                    dve.wait_ge(*upto(wx, u, j))
                    ti.carry(dve, u, j)

            def turn(j, more):
                dve.wait_ge(*upto(ti.summed[1], U - 1, j))
                for u in range(U):
                    dve.wait_ge(*upto(x_in, u, j, inc=32))
                    V.tensor_tensor(ti.halves(Y[u][:]), ti.total(u), ti.halves(X[u][:, 0, :]), ALU.add).then_inc(y_ready[u], 1)
                    ln_stats(net, dve, chain, j, S, lambda u: dve.wait_ge(*upto(y_ready, u, j)),
                             lambda u: [Y[u][:], X[u][:, 1, :]], var, slots=[u])
                if more:
                    messages(j + 1)
            turns_ahead(dve, TURNS, messages, turn)


def edge_mlp(net):
    nc, a, D, C, T = net.nc, net.a, net.D, net.C, net.T
    U, TURNS = 4, T // 4
    with Stage(nc) as st:
        X = st.sb("g_x", [P, D], n=U)
        I = st.sb("g_i", [P, 1], I32, n=U)
        A = st.sb("g_attr", [net.DE, P], n=U)
        XT = st.sb("g_xt", [P, C, P], n=2)
        RL = st.sb("g_relu", [P, C, P], n=2)
        SG = st.sb("g_gate", [P, D], n=2)
        M = st.sb("g_msg", [P, D], n=2)
        idx, got, ea, tp, xt, hid, relu, gate, sg, core, msg, stored = (st.sem(f"g_{n}", U) for n in (
            "index_ready", "gathered", "attr_loaded", "transposed", "xt_ready", "hidden", "relu_ready", "gate_ready", "sigmoid_ready",
            "core_ready", "msg_ready", "stored"))
        tps, hds, gts, crs = (st.ps(f"g_ps_{n}", 2) for n in ("t", "h", "g", "c"))
        bias = st.sb("g_bias", [P, 2, D])
        GB = st.sb("g_gate_biased", [P, D], n=2)
        CB = st.sb("g_core_biased", [P, D], n=2)
        bias_in = st.sem("g_bias_loaded")
        g_biased, c_biased = st.sem("g_gate_biased", U), st.sem("g_core_biased", U)
        block = st.ctx.enter_context(nc.Block())

        @block.sync
        def _(sp):
            def load(j, u):
                sp.wait_ge(*upto(gate, u, j, back=U))
                sp.dma_start(A[u][:], a["edge_attr_t"][:, bass.ds((j * U + u) * P, P)]).then_inc(ea[u], 16)

            def store(j, u):
                sp.wait_ge(*upto(msg, u, j))
                sp.dma_start(tile_of(net.msg, j * U + u), M[u % 2][:]).then_inc(stored[u], 16)
            for k, name in enumerate(("bg", "bm2")):
                sp.dma_start(bias[:, k, :], a[name].partition_broadcast(P)).then_inc(bias_in, 16)
            load_store(sp, TURNS, U, load, store)
            for u in range(U):
                sp.wait_ge(stored[u], 16 * TURNS)

        @block.gpsimd
        def _(gp):
            with gp.Fori(0, TURNS) as j:
                for u in range(U):
                    hold(net, gp, *upto(tp, u, j, back=U))
                    nc.gpsimd.tensor_copy(I[u][:], col(net.table_row, j * U + u)).then_inc(idx[u], 1)
                    hold(net, gp, *upto(idx, u, j))
                    gather(net, X[u][:], net.x2, I[u][:]).then_inc(got[u], 16)

        @block.tensor
        def _(pe):
            def transposes(j, u):
                b = u % 2
                pe.wait_ge(*upto(got, u, j, inc=16))
                pe.wait_ge(*upto(xt, u, j, back=2))
                for c in range(C):
                    mm = nc.tensor.transpose(tps[b][:, c * P:(c + 1) * P], X[u][:, c * P:(c + 1) * P], net.ident[:])
                mm.then_inc(tp[u], 1)

            def layers(j, u):
                b = u % 2
                pe.wait_ge(*upto(xt, u, j))
                pe.wait_ge(*upto(ea, u, j, inc=16))
                pe.wait_ge(*upto(relu, u, j, back=2))
                for m in range(C):
                    for c in range(C):
                        nc.tensor.matmul(hds[b][:, m * P:(m + 1) * P], net.w_m1[:, c, m * P:(m + 1) * P], XT[b][:, c, :], start=c == 0, stop=False)
                    mm = nc.tensor.matmul(hds[b][:, m * P:(m + 1) * P], net.w_m1e[:, m * P:(m + 1) * P], A[u][:], start=False, stop=True)
                mm.then_inc(hid[u], 1)
                pe.wait_ge(*upto(g_biased, u, j, back=2))
                for c in range(C):
                    nc.tensor.matmul(gts[b][:, 0:D], XT[b][:, c, :], net.w_g[:, c, :], start=c == 0, stop=False)
                nc.tensor.matmul(gts[b][:, 0:D], A[u][:], net.w_ge[:], start=False, stop=True).then_inc(gate[u], 1)
                pe.wait_ge(*upto(relu, u, j))
                pe.wait_ge(*upto(c_biased, u, j, back=2))
                for c in range(C):
                    mm = nc.tensor.matmul(crs[b][:, 0:D], RL[b][:, c, :], net.w_m2[:, c, :], start=c == 0, stop=c == C - 1)
                mm.then_inc(core[u], 1)

            def turn(j, more):
                for u in range(U):
                    if more or u + 1 < U:
                        transposes(*following(U, j, u))
                    layers(j, u)
            turns_ahead(pe, TURNS, lambda j: transposes(j, 0), turn)

        @block.scalar
        def _(act):
            def move(j, u):
                b = u % 2
                act.wait_ge(*upto(tp, u, j))
                act.wait_ge(*upto(gate, u, j, back=2))
                nc.scalar.activation(XT[b][:].rearrange("p k e -> p (k e)"), tps[b][:, 0:D], ACT.Copy).then_inc(xt[u], 1)

            def relu_gate(j, u):
                b = u % 2
                act.wait_ge(*upto(hid, u, j))
                act.wait_ge(*upto(core, u, j, back=2))
                for m in range(C):
                    mv = nc.scalar.activation(RL[b][:, m, :], hds[b][:, m * P:(m + 1) * P], ACT.Relu, bias=net.cols[:, 1, m:m + 1])
                mv.then_inc(relu[u], 1)
                act.wait_ge(*upto(g_biased, u, j))
                act.wait_ge(*upto(msg, u, j, back=2))
                nc.scalar.activation(SG[b][:], GB[b][:], ACT.Sigmoid).then_inc(sg[u], 1)

            def turn(j, more):
                for u in range(U):
                    if more or u + 1 < U:
                        move(*following(U, j, u))
                    relu_gate(j, u)
            turns_ahead(act, TURNS, lambda j: move(j, 0), turn)

        @block.vector
        def _(dve):
            dve.wait_ge(bias_in, 32)
            with dve.Fori(0, TURNS) as j:
                for u in range(U):
                    b = u % 2
                    dve.wait_ge(*upto(gate, u, j))
                    dve.wait_ge(*upto(sg, u, j, back=2))
                    nc.vector.tensor_tensor(GB[b][:], gts[b][:, 0:D], bias[:, 0, :], ALU.add).then_inc(g_biased[u], 1)
                    dve.wait_ge(*upto(core, u, j))
                    dve.wait_ge(*upto(msg, u, j, back=2))
                    nc.vector.tensor_tensor(CB[b][:], crs[b][:, 0:D], bias[:, 1, :], ALU.add).then_inc(c_biased[u], 1)
                    dve.wait_ge(*upto(c_biased, u, j))
                    dve.wait_ge(*upto(sg, u, j))
                    dve.wait_ge(*upto(stored, u, j, back=2, inc=16))
                    nc.vector.tensor_tensor(M[b][:], CB[b][:], SG[b][:], ALU.mult).then_inc(msg[u], 1)


def mlp_sum(net):
    nc, D, C, T = net.nc, net.D, net.C, net.T
    U, TURNS = 4, T // 4
    with Stage(nc) as st:
        ti = Tiles(net, st, n=U)
        X = st.sb("h_x", [P, 2, D], n=U)
        B = st.sb("h_b", [P, 2, D], n=U)
        Y = st.sb("h_y", [P, D], n=U)
        Z = st.sb("h_z", [P, 2, D], n=U)
        X3 = st.sb("h_x3", [P, 2, D], n=U)
        XT = st.sb("h_xt", [P, 4, P], n=U)
        HH = st.sb("h_h", [P, 2, D], n=U)
        S = st.sb("h_small", [P, 64], n=U)
        (x_in, xb, m_ready, y_ready, var1, dev1, nrm, scaled, z_ready, var2, dev2, x3_ready, tp, xt, pr, silu, stored, chain1, chain2) = (
            st.sem(f"h_{n}", U) for n in (
                "loaded", "x_biased", "messages_in", "y_ready", "var1_ready", "dev1_ready", "normed", "scaled", "z_ready", "var2_ready",
                "dev2_ready", "x3_ready", "transposed", "xt_ready", "projected", "silu_ready", "stored", "dve_chain1", "dve_chain2"))
        shift = st.sem("h_shift_ready", U)
        m_in = st.sem("h_messages_loaded", U)
        tps, prs = (st.ps(f"h_ps_{n}", 2) for n in ("t", "p"))
        block = st.ctx.enter_context(nc.Block())

        @block.sync
        def _(sp):
            def load(j, u):
                t = j * U + u
                hold(net, sp, *upto(ti.summed[1], u, j, back=U))
                sp.dma_start(ti.msg[u][:], tile_of(net.msg, t)).then_inc(m_in[u], 16)
                sp.dma_start(ti.keys[u][:], keys_of(net, t)).then_inc(m_in[u], 16)

            def load_x(j, u):
                t = j * U + u
                hold(net, sp, *upto(xb, u, j, back=U, inc=2))
                hold(net, sp, *upto(scaled, u, j, back=U))
                for i in range(2):
                    sp.dma_start(X[u][:, i, :], rows2(net, net.x2, t, i)).then_inc(x_in[u], 16)

            with sp.Fori(0, TURNS) as j:
                for part in (load, load_x):
                    for u in range(U):
                        part(j, u)

        @block.gpsimd
        def _(gp):
            with gp.Fori(0, TURNS) as j:
                for u in range(U):
                    gp.wait_ge(*upto(z_ready, u, j, back=U))
                    hold(net, gp, *upto(x_in, u, j, inc=32))
                    for i in range(2):
                        nc.gpsimd.tensor_tensor(B[u][:, i, :], X[u][:, i, :], net.bc["beta"][:], ALU.add).then_inc(xb[u], 1)
                for u in range(U):
                    hold(net, gp, *upto(var1, u, j))
                    inv_dev(net, S[u], 2).then_inc(dev1[u], 1)
                for u in range(U):
                    hold(net, gp, *upto(var2, u, j))
                    dev_shift(net, gp, S[u], 2, dev2[u], shift[u], upto(dev2, u, j)[1])

        @block.tensor
        def _(pe):
            def sums(j):
                for u in range(U):
                    ti.sum_pe(pe, u, j)

            def turn(j, more):
                if more:
                    sums(j + 1)
                for u in range(U):
                    pe.wait_ge(*upto(x3_ready, u, j, inc=2))
                    pe.wait_ge(*upto(xt, u, j, back=2))
                    for k in range(4):
                        mm = nc.tensor.transpose(tps[u % 2][:, k * P:(k + 1) * P], X3[u][:, k // 2, (k % 2) * P:(k % 2 + 1) * P], net.ident[:])
                    mm.then_inc(tp[u], 1)
                for u in range(U):
                    pe.wait_ge(*upto(xt, u, j))
                    pe.wait_ge(*upto(silu, u, j, back=2))
                    for i in range(2):
                        for c in range(C):
                            nc.tensor.matmul(prs[u % 2][:, i * D:(i + 1) * D], XT[u][:, 2 * i + c, :], net.w_in[:, c, :], start=c == 0, stop=False)
                        mm = nc.tensor.matmul(prs[u % 2][:, i * D:(i + 1) * D], net.ones[0:1, :], net.rows1[:, 0, :], start=False, stop=True)
                    mm.then_inc(pr[u], 1)
            turns_ahead(pe, TURNS, sums, turn)

        @block.scalar
        def _(act):
            def move(j, u):
                act.wait_ge(*upto(tp, u, j))
                act.wait_ge(*upto(pr, u, j, back=U))
                nc.scalar.activation(XT[u][:].rearrange("p k e -> p (k e)"), tps[u % 2][:, :], ACT.Copy).then_inc(xt[u], 1)
                act.dma_start(tile_of(net.x3, j * U + u), X3[u][:, 0, :]).then_inc(stored[u], 16)

            with act.Fori(0, TURNS) as j:
                for u in range(U):
                    act.wait_ge(*upto(shift, u, j))
                    act.wait_ge(*upto(tp, u, j, back=U))
                    act.wait_ge(*upto(stored, u, j, back=U, inc=48))
                    for i in range(2):
                        normed_act(net, X3[u][:, i, :], Z[u][:, i, :], S[u], i).then_inc(x3_ready[u], 1)
                    if u:
                        move(j, u - 1)
                move(j, U - 1)
                for u in range(U):
                    act.wait_ge(*upto(pr, u, j))
                    act.wait_ge(*upto(stored, u, j, back=U, inc=48))
                    nc.scalar.activation(HH[u][:].rearrange("p a d -> p (a d)"), prs[u % 2][:, :], ACT.Silu).then_inc(silu[u], 1)
                    act.wait_ge(*upto(silu, u, j))
                    for i in range(2):
                        act.dma_start(rows2(net, net.h, j * U + u, i), HH[u][:, i, :]).then_inc(stored[u], 16)
            for u in range(U):
                act.wait_ge(stored[u], 48 * TURNS)

        @block.vector
        def _(dve):
            V = nc.vector
            ti.start(dve)

            def messages(j):
                for u in range(U):
                    dve.wait_ge(*upto(m_in, u, j, inc=32))
                    ti.equal(dve, u, j)
                    ti.carry(dve, u, j)

            def turn(j, more):
                dve.wait_ge(*upto(ti.summed[1], U - 1, j))
                for u in range(U):
                    dve.wait_ge(*upto(x_in, u, j, inc=32))
                    V.tensor_tensor(ti.halves(Y[u][:]), ti.total(u), ti.halves(X[u][:, 0, :]), ALU.add).then_inc(y_ready[u], 1)

                def y_in(u):
                    dve.wait_ge(*upto(y_ready, u, j))
                    dve.wait_ge(*upto(x3_ready, u, j, back=U, inc=2))
                ln_stats(net, dve, chain1, j, S, y_in, lambda u: [Y[u][:], X[u][:, 1, :]], var1)
                for u in range(U):
                    dve.wait_ge(*upto(dev1, u, j))
                    normed(net, Z[u][:, 0, :], Y[u][:], S[u], 0)
                    normed(net, Z[u][:, 1, :], X[u][:, 1, :], S[u], 1).then_inc(nrm[u], 1)
                for u in range(U):
                    dve.wait_ge(*upto(nrm, u, j))
                    V.tensor_tensor(Z[u][:], Z[u][:], net.bc["gamma"][:].unsqueeze(1).broadcast_to([P, 2, D]), ALU.mult).then_inc(scaled[u], 1)
                for u in range(U):
                    dve.wait_ge(*upto(xb, u, j, inc=2))
                    dve.wait_ge(*upto(scaled, u, j))
                    V.tensor_tensor(Z[u][:], Z[u][:], B[u][:], ALU.add).then_inc(z_ready[u], 1)
                ln_stats(net, dve, chain2, j, S, lambda u: dve.wait_ge(*upto(z_ready, u, j)),
                             lambda u: [Z[u][:, i, :] for i in range(2)], var2)
                if more:
                    messages(j + 1)
            turns_ahead(dve, TURNS, messages, turn)


def diffuse(net, acc, step):
    nc, D, T, R = net.nc, net.D, net.T, net.R
    U, TURNS = 4, T // 4
    rows, src = (net.table_row, net.h) if step == 1 else (net.term_row, net.term[step % 2])
    dst = net.term[(step + 1) % 2]
    with Stage(nc) as st:
        ti = Tiles(net, st, n=U, apart=True)
        I = st.sb("i_i", [P, 1], I32, n=U)
        TM = st.sb("i_term", [P, D], n=U)
        scale = st.sb("i_scale", [P, T])
        acc_in, sc_ready = st.sem("i_acc_loaded"), st.sem("i_scale_ready")
        idx, got, k_in, term, added, stored = (st.sem(f"i_{n}", U) for n in (
            "index_ready", "gathered", "keys_loaded", "term_ready", "added", "stored"))
        block = st.ctx.enter_context(nc.Block())

        @block.sync
        def _(sp):
            if step == 1:
                sp.dma_start(acc[:], net.h[0:R, :].rearrange("(t p) d -> p t d", p=P)).then_inc(acc_in, 16)

            def load(j, u):
                sp.wait_ge(*upto(ti.eq_ready, u, j, back=U))
                sp.dma_start(ti.keys[u][:], keys_of(net, j * U + u)).then_inc(k_in[u], 16)
            with sp.Fori(0, TURNS) as j:
                for u in range(U):
                    load(j, u)

        @block.gpsimd
        def _(gp):
            with gp.Fori(0, TURNS) as j:
                for u in range(U):
                    hold(net, gp, *upto(ti.summed[1], u, j, back=U))
                    nc.gpsimd.tensor_copy(I[u][:], col(rows, j * U + u)).then_inc(idx[u], 1)
                    hold(net, gp, *upto(idx, u, j))
                    gather(net, ti.msg[u][:], src, I[u][:]).then_inc(got[u], 16)

        @block.tensor
        def _(pe):
            with pe.Fori(0, TURNS) as j:
                for u in range(U):
                    pe.wait_ge(*upto(term, u, j, back=U))
                    ti.sum_pe(pe, u, j)

        @block.scalar
        def _(act):
            nc.scalar.activation(scale[:], net.inv_deg[:], ACT.Copy, scale=1.0 / step).then_inc(sc_ready, 1)
            act.wait_ge(sc_ready, 1)
            with act.Fori(0, TURNS) as j:
                for u in range(U):
                    act.wait_ge(ti.msg_ready[1][(u + 1) % U], j + 1 + (u == U - 1))
                    if step < STEPS:
                        act.wait_ge(*upto(stored, u, j, back=U, inc=16))
                    act.wait_ge(*upto(added, u, j, back=U))
                    for s in range(2):
                        mv = nc.scalar.activation(TM[u][:, s * ti.w:(s + 1) * ti.w], ti.half(s, u), ACT.Copy, scale=col(scale, j * U + u))
                    mv.then_inc(term[u], 1)
                    if step < STEPS:
                        act.wait_ge(*upto(term, u, j))
                        act.dma_start(dst[bass.ds((j * U + u) * P, P), :], TM[u][:]).then_inc(stored[u], 16)
            if step < STEPS:
                for u in range(U):
                    act.wait_ge(stored[u], 16 * TURNS)

        @block.vector
        def _(dve):
            V = nc.vector

            def messages(j, u):
                dve.wait_ge(*upto(k_in, u, j, inc=16))
                ti.equal(dve, u, j).then_inc(ti.eq_ready[u], 1)
                dve.wait_ge(*upto(got, u, j, inc=16))
                ti.carry(dve, u, j)

            def body(j, last=False):
                for u in range(U):
                    if u + 2 < U:
                        messages(j, u + 2)
                    elif not last:
                        messages(j + 1, u + 2 - U)
                    elif u == U - 1:
                        dve.wait_ge(ti.summed[1][u], TURNS)
                        dve.sem_inc(ti.msg_ready[1][0], 1)
                    dve.wait_ge(*upto(term, u, j))
                    row = acc[:, bass.ds(j * U + u, 1), :].rearrange("p o d -> p (o d)")
                    V.tensor_tensor(row, row, TM[u][:], ALU.add).then_inc(added[u], 1)
            ti.start(dve)
            if step == 1:
                dve.wait_ge(acc_in, 16)
            messages(0, 0)
            messages(0, 1)
            with dve.Fori(0, TURNS - 1) as j:
                body(j)
            body(TURNS - 1, last=True)


def output(net, acc):
    nc, a, D, C, T, N = net.nc, net.a, net.D, net.C, net.T, net.N
    U, TURNS = 4, T // 4
    with Stage(nc) as st:
        A = st.sb("j_a", [P, D], n=U)
        X = st.sb("j_x", [P, D], n=U)
        XT = st.sb("j_xt", [P, C, P], n=U)
        Y = st.sb("j_y", [P, D], n=U)
        O = st.sb("j_o", [P, D], n=U)
        I = st.sb("j_i", [P, 1], I32, n=U)
        S = st.sb("j_small", [P, 64], n=U)
        x_in, xb, acc_ready, tp, xt, pr, y_ready, var, dev, o_ready, idx, stored, chain = (st.sem(f"j_{n}", U) for n in (
            "loaded", "x_biased", "acc_ready", "transposed", "xt_ready", "projected", "y_ready", "var_ready", "dev_ready", "out_ready",
            "index_ready", "stored", "dve_chain"))
        tps, prs = (st.ps(f"j_ps_{n}", U) for n in ("t", "p"))
        block = st.ctx.enter_context(nc.Block())

        @block.sync
        def _(sp):
            with sp.Fori(0, TURNS) as j:
                for u in range(U):
                    sp.wait_ge(*upto(y_ready, u, j, back=U))
                    sp.dma_start(X[u][:], tile_of(net.x3, j * U + u)).then_inc(x_in[u], 16)

        @block.gpsimd
        def _(gp):
            with gp.Fori(0, TURNS) as j:
                for u in range(U):
                    hold(net, gp, *upto(var, u, j))
                    inv_dev(net, S[u], 1).then_inc(dev[u], 1)
                for u in range(U):
                    gp.wait_ge(*upto(o_ready, u, j))
                    hold(net, gp, *upto(stored, u, j, back=U, inc=16))
                    nc.gpsimd.tensor_copy(I[u][:], col(net.rep_node, j * U + u)).then_inc(idx[u], 1)
                    hold(net, gp, *upto(idx, u, j))
                    nc.gpsimd.indirect_dma_start(a["out"], bass.IndirectOffsetOnAxis(I[u][:], 0), O[u][:], None,
                                                 bounds_check=N - 1, oob_is_err=False).then_inc(stored[u], 16)
            for u in range(U):
                gp.wait_ge(stored[u], 16 * TURNS)

        @block.tensor
        def _(pe):
            with pe.Fori(0, TURNS) as j:
                for u in range(U):
                    pe.wait_ge(*upto(acc_ready, u, j))
                    pe.wait_ge(*upto(xt, u, j, back=U))
                    for c in range(C):
                        mm = nc.tensor.transpose(tps[u][:, c * P:(c + 1) * P], A[u][:, c * P:(c + 1) * P], net.ident[:])
                    mm.then_inc(tp[u], 1)
                for u in range(U):
                    pe.wait_ge(*upto(xt, u, j))
                    pe.wait_ge(*upto(y_ready, u, j, back=U))
                    for c in range(C):
                        mm = nc.tensor.matmul(prs[u][:, 0:D], XT[u][:, c, :], net.w_out[:, c, :], start=c == 0, stop=c == C - 1)
                    mm.then_inc(pr[u], 1)

        @block.scalar
        def _(act):
            with act.Fori(0, TURNS) as j:
                for u in range(U):
                    act.wait_ge(*upto(tp, u, j, back=U))
                    nc.scalar.activation(A[u][:], acc[:, bass.ds(j * U + u, 1), :].rearrange("p o d -> p (o d)"), ACT.Copy).then_inc(acc_ready[u], 1)
                for u in range(U):
                    act.wait_ge(*upto(tp, u, j))
                    act.wait_ge(*upto(pr, u, j, back=U))
                    nc.scalar.activation(XT[u][:].rearrange("p k e -> p (k e)"), tps[u][:, 0:D], ACT.Copy).then_inc(xt[u], 1)

        @block.vector
        def _(dve):
            V = nc.vector
            with dve.Fori(0, TURNS) as j:
                for u in range(U):
                    dve.wait_ge(*upto(x_in, u, j, inc=16))
                    V.tensor_tensor(X[u][:], X[u][:], net.bc["b_out"][:], ALU.add).then_inc(xb[u], 1)
                for u in range(U):
                    dve.wait_ge(*upto(pr, u, j))
                    dve.wait_ge(*upto(xb, u, j))
                    V.tensor_tensor(Y[u][:], prs[u][:, 0:D], X[u][:], ALU.add).then_inc(y_ready[u], 1)
                ln_stats(net, dve, chain, j, S, lambda u: dve.wait_ge(*upto(y_ready, u, j)), lambda u: [Y[u][:]], var)
                for u in range(U):
                    dve.wait_ge(*upto(dev, u, j))
                    dve.wait_ge(*upto(stored, u, j, back=U, inc=16))
                    normed(net, O[u][:], Y[u][:], S[u], 0).then_inc(o_ready[u], 1)


def build(nc, a):
    with ExitStack() as ctx:
        net = Net(nc, a, ctx)
        setup(net)
        dense(net)
        project1(net)
        softmax(net, 1)
        gat1(net)
        gather_out1(net)
        softmax(net, 2)
        gat2(net)
        project_qkv(net)
        softmax(net, 3)
        attend(net)
        edge_mlp(net)
        mlp_sum(net)
        acc = ctx.enter_context(nc.sbuf_tensor("acc", [P, net.T, net.D], F32))
        for step in range(1, STEPS + 1):
            diffuse(net, acc, step)
        output(net, acc)


def layouts(x, src, dst, edge_attr):
    N, E = x.shape[0], src.shape[0]
    T = -(-E // (P - 1))
    T += -T % 4
    pad = T * (P - 1) - E
    tiles = lambda v, fill: np.concatenate([v, np.full(pad, fill, v.dtype)]).reshape(T, P - 1)
    key = tiles(dst, N)
    before = np.concatenate([np.full((1, 1), -1, dst.dtype), key[:-1, -1:]])
    behind = np.concatenate([key[1:, :1], np.full((1, 1), -1, dst.dtype)])
    slot = lambda v: np.concatenate([v[:, :1], v], axis=1)
    index = np.stack([slot(tiles(src, 0)).T, slot(tiles(dst, 0)).T], axis=2)
    attr = np.concatenate([edge_attr, np.zeros((pad, edge_attr.shape[1]), edge_attr.dtype)]).reshape(T, P - 1, -1)
    attr = np.concatenate([np.zeros((T, 1, attr.shape[2]), attr.dtype), attr], axis=1)
    return {
        "key_rows": np.concatenate([before, key, behind], axis=1),
        "key_in_cols": np.concatenate([before, key], axis=1).T,
        "key_out": np.concatenate([key[:, -1:], key], axis=1),
        "index_cols": index,
        "edge_attr_t": attr.reshape(T * P, -1).T,
    }


def arrays_of(inputs):
    i = {k: np.asarray(v) for k, v in inputs.items()}
    D = i["x"].shape[1]
    flat = lambda n: i[n].reshape(-1)
    return {
        "x": i["x"],
        **layouts(i["x"], i["src"], i["dst"], i["edge_attr_64"]),
        "w1": i["L0_gnn_W1"].reshape(D, D), "w2": i["L0_gnn_W2"].reshape(D, D),
        "a_src1": flat("L0_gnn_a_src1"), "a_dst1": flat("L0_gnn_a_dst1"), "b1": i["L0_gnn_b1"],
        "a_src2": flat("L0_gnn_a_src2"), "a_dst2": flat("L0_gnn_a_dst2"), "b2": i["L0_gnn_b2"],
        "wq": i["L1_gnn_Wq"], "bq": i["L1_gnn_bq"], "wk": i["L1_gnn_Wk"], "bk": i["L1_gnn_bk"], "wv": i["L1_gnn_Wv"], "bv": i["L1_gnn_bv"],
        "wm1": i["L2_gnn_W1"], "bm1": i["L2_gnn_b1"], "wm2": i["L2_gnn_W2"], "bm2": i["L2_gnn_b2"], "wg": i["L2_gnn_Wg"], "bg": i["L2_gnn_bg"],
        "gamma": i["L2_gnn_gamma"], "beta": i["L2_gnn_beta"],
        "w_in_t": i["L3_gnn_W_in"].T, "b_in": i["L3_gnn_b_in"], "w_out_t": i["L3_gnn_W_out"].T, "b_out": i["L3_gnn_b_out"],
    }


def program(nc, arrays):
    a = {n: nc.dram_tensor(f"in_{n}", v.shape, mybir.dt.from_np(v.dtype), kind="ExternalInput").ap() for n, v in arrays.items()}
    a["out"] = nc.dram_tensor("out", list(arrays["x"].shape), F32, kind="ExternalOutput").ap()
    build(nc, a)


def kernel(**inputs):
    import concourse.bacc as bacc
    from concourse.bass_utils import run_bass_kernel_spmd

    arrays = {n: np.ascontiguousarray(v) for n, v in arrays_of(inputs).items()}
    nc = bacc.Bacc("TRN2", target_bir_lowering=False, num_devices=1)
    program(nc, arrays)
    r = run_bass_kernel_spmd(nc, [{f"in_{n}": v for n, v in arrays.items()}], core_ids=[0])
    return r.results[0]["out"]
```
